# Optimizing a Trainium2 kernel written in Bass

```python
import numpy as np
import jax
import jax.numpy as jnp

def _softmax(x, axis=-1):
    return jax.nn.softmax(x, axis=axis)

def _gelu(x):
    return jax.nn.gelu(x, approximate=True)

def _silu(x):
    return jax.nn.silu(x)

def _sigmoid(x):
    return jax.nn.sigmoid(x)

def _layernorm(x, axis=-1, eps=1e-05):
    m = jnp.mean(x, axis=axis, keepdims=True)
    v = jnp.var(x, axis=axis, keepdims=True)
    return (x - m) / jnp.sqrt(v + eps)

def _scatter_add(tgt, idx, src, axis=0):
    return tgt.at[idx].add(src)

def _segment_sum(src, seg, n):
    return jax.ops.segment_sum(src, seg, n)
kernel_name = 'mk_flamingo_gated_d1_seqx_r4_a87c01'

def setup_inputs(seed: int=0):
    np.random.seed(seed)
    _w = jnp.asarray

    def _rec_inputs():
        import jax
        import jax.numpy as jnp
        _rk = jax.random.key(seed)
        x = -0.0003929 + 0.9999 * jax.random.normal(jax.random.fold_in(_rk, 1), (4, 1024, 256), jnp.float32)
        _lenS = 1024 - jax.random.randint(jax.random.fold_in(_rk, 7), (4,), 0, max(1, 1024 // 4) + 1, jnp.int32)
        _lenS2 = 64 - jax.random.randint(jax.random.fold_in(_rk, 8), (4,), 0, max(1, 64 // 4) + 1, jnp.int32)
        _ctx_1024P = jax.random.normal(jax.random.fold_in(_rk, 11), (4, 16, 256), jnp.float32)
        _ctx_1024c = jax.random.dirichlet(jax.random.fold_in(_rk, 511), 0.3 * jnp.ones((16,), jnp.float32), (4, 64))
        _ctx_1024t = jnp.einsum('bsk,bkd->bsd', _ctx_1024c, _ctx_1024P)
        _ctx_1024t = _ctx_1024t * jax.lax.rsqrt(jnp.mean(jnp.square(_ctx_1024t)) + 1e-12) * 0.953939
        ctx_1024 = 2.81802e-05 + 1.00001 * (_ctx_1024t + 0.3 * jax.random.normal(jax.random.fold_in(_rk, 611), (4, 64, 256), jnp.float32))
        _g = jax.random.normal(jax.random.fold_in(_rk, 9001), (2, 1), jnp.float32)
        _g = jnp.sign(_g) * jnp.maximum(jnp.abs(_g), 1.0) + (_g == 0) * 1.0
        g_xattn = _g[0]
        g_ffn = _g[1]
        return (x, ctx_1024, g_xattn, g_ffn)
    x, ctx_1024, g_xattn, g_ffn = _rec_inputs()

    def _L0_xattn_setup():
        import jax, jax.numpy as jnp
        import numpy as np
        key = jax.random.key(seed)
        k1, k2, k3 = jax.random.split(key, 3)
        B, L, D = (8, 512, 256)
        ix = jax.random.normal(k1, (B, L, D), dtype=jnp.float32)
        iother = jax.random.normal(k2, (B, L, D), dtype=jnp.float32)
        W = jax.random.normal(k3, (D, D), dtype=jnp.float32) * (1.0 / np.sqrt(D))
        b = jnp.zeros((D,), dtype=jnp.float32)
        return {'ix': ix, 'iother': iother, 'W': W, 'b': b}
    _L0_xattn_all = _L0_xattn_setup()
    _L0_xattn_in = {k: v for k, v in _L0_xattn_all.items() if k in ('W', 'b')}
    del _L0_xattn_all

    def _L0_ffn_setup():
        import jax, jax.numpy as jnp
        import numpy as np
        DIM = 256
        HIDDEN = 768
        SCALE = 1.0 / 127.0

        def _dequant(w_int, dtype):
            return w_int.astype(dtype) * jnp.asarray(SCALE, dtype)
        key = jax.random.key(seed)
        k_x, k_g, k_u, k_d = jax.random.split(key, 4)
        x = jax.random.normal(k_x, (4, 512, DIM), dtype=jnp.float32)
        w_gate = jax.random.randint(k_g, (HIDDEN, DIM), -127, 128, dtype=jnp.int32)
        w_up = jax.random.randint(k_u, (HIDDEN, DIM), -127, 128, dtype=jnp.int32)
        w_down = jax.random.randint(k_d, (DIM, HIDDEN), -127, 128, dtype=jnp.int32)
        return {'x': x, 'w_gate': w_gate, 'w_up': w_up, 'w_down': w_down}
    _L0_ffn_all = _L0_ffn_setup()
    _L0_ffn_in = {k: v for k, v in _L0_ffn_all.items() if k in ('w_gate', 'w_up', 'w_down')}
    del _L0_ffn_all
    return {'x': x, 'ctx_1024': ctx_1024, 'g_xattn': g_xattn, 'g_ffn': g_ffn, 'L0_xattn_W': _L0_xattn_in['W'], 'L0_xattn_b': _L0_xattn_in['b'], 'L0_ffn_w_gate': _L0_ffn_in['w_gate'], 'L0_ffn_w_up': _L0_ffn_in['w_up'], 'L0_ffn_w_down': _L0_ffn_in['w_down']}

def reference(x, ctx_1024, g_xattn, g_ffn, L0_xattn_W, L0_xattn_b, L0_ffn_w_gate, L0_ffn_w_up, L0_ffn_w_down):
    import jax
    import jax.numpy as jnp

    def _L0_xattn_ref(ix, iother, W, b):
        import jax, jax.numpy as jnp
        import numpy as np
        ex = ix @ W.T + b
        eother = iother @ W.T + b
        align = jnp.einsum('bld,bmd->blm', ex, eother)
        align = jax.nn.softmax(align, axis=-1)
        aligned = jnp.einsum('blm,bmd->bld', align, iother)
        return aligned

    def _L0_ffn_ref(x, w_gate, w_up, w_down):
        import jax, jax.numpy as jnp
        import numpy as np
        DIM = 256
        HIDDEN = 768
        SCALE = 1.0 / 127.0

        def _dequant(w_int, dtype):
            return w_int.astype(dtype) * jnp.asarray(SCALE, dtype)
        wg = _dequant(w_gate, x.dtype)
        wu = _dequant(w_up, x.dtype)
        wd = _dequant(w_down, x.dtype)
        gate = jnp.einsum('bsd,hd->bsh', x, wg)
        up = jnp.einsum('bsd,hd->bsh', x, wu)
        h = jax.nn.silu(gate) * up
        return jnp.einsum('bsh,dh->bsd', h, wd)
    x = x + jnp.tanh(g_xattn[0]) * _L0_xattn_ref(_layernorm(x, axis=-1), ctx_1024, L0_xattn_W, L0_xattn_b)
    x = x + jnp.tanh(g_ffn[0]) * _L0_ffn_ref(_layernorm(x, axis=-1), L0_ffn_w_gate, L0_ffn_w_up, L0_ffn_w_down)
    return x

_drawn_inputs = setup_inputs


def setup_inputs(seed=0):
    import zlib

    import numpy as np

    out = dict(_drawn_inputs(seed))
    spreads = {'L0_xattn_b': (0.0, 0.1)}
    factors = {}
    for name, (base, spread) in spreads.items():
        noise = np.random.default_rng([zlib.crc32(name.encode()), seed]).standard_normal(out[name].shape)
        drawn = base * np.exp(spread * noise) if base else spread * noise
        out[name] = jnp.asarray(drawn.astype(out[name].dtype))
    for name, factor in factors.items():
        out[name] = (out[name] * factor).astype(out[name].dtype)
    return out
```

```python
from contextlib import ExitStack

import concourse.bass as bass
from concourse import mybir

F32 = mybir.dt.float32
F32R = mybir.dt.float32r
F16 = mybir.dt.float16
I32 = mybir.dt.int32
ALU = mybir.AluOpType
ACT = mybir.ActivationFunctionType
AX = mybir.AxisListType

P = 128
TILES = 4
BLOCK = TILES * P
EPS = 1e-5
RSQRT_MAGIC = float(0x5F3759DF)
NEWTON = 3
LN_OPS = 8 + 3 * NEWTON
LN_SCALE = 2048.0
H_SCALE = 0.5
QUANT = 127.0


def gated_cross_attention_and_ffn(nc, x, ctx, g_xattn, g_ffn, W, b, w_gate, w_up, w_down, out):
    B, S, D = x.shape
    M = ctx.shape[1]
    HID = w_gate.shape[0]
    DC = D // P
    HC = HID // P
    BLOCKS = B * S // BLOCK
    ROWS = B * M
    RC = ROWS // P
    assert DC == 2 and RC == 2 and TILES * M <= 512 and S == 2 * BLOCK and HC == 6 and D <= 512

    x_v = x.rearrange("b s d -> (b s) d").rearrange("(k p j) d -> k p (j d)", p=P, j=TILES)
    out_v = out.rearrange("b s d -> (b s) d").rearrange("(k p j) d -> k p (j d)", p=P, j=TILES)

    with ExitStack() as stack:
        def sb(name, shape, dt):
            return stack.enter_context(nc.sbuf_tensor(name, shape, dt))

        def psum(name):
            return stack.enter_context(nc.psum_tensor(name, [P, 512], F32))

        def sem(name):
            return stack.enter_context(nc.semaphore(name))

        xs = sb("xs", [P, BLOCKS * TILES * D], F32)
        ident = sb("ident", [P, P], F32)
        ident16 = sb("ident16", [P, P], F16)
        W_nat = sb("W_nat", [P, DC, D], F32)
        W_T = sb("W_T", [P, DC, D], F32)
        b_col = sb("b_col", [P, DC], F32)
        b_rep = sb("b_rep", [P, DC, P], F32)
        ctx_nat = sb("ctx_nat", [P, RC, D], F32)
        ctx_T = sb("ctx_T", [P, DC, ROWS], F32)
        ctx_m = sb("ctx_m", [2 * M, B * D], F32)
        ctx_hi = sb("ctx_hi", [2 * M, B * D], F32R)
        ctx_lo = sb("ctx_lo", [2 * M, B * D], F32R)
        eo_T = sb("eo_T", [P, DC, ROWS], F32)
        key_T = sb("key_T", [P, DC, ROWS], F32)
        b_dot = sb("b_dot", [P, ROWS], F32)
        g_raw = sb("g_raw", [P, 2], F32)
        g_tanh = sb("g_tanh", [P, 2], F32)
        out_coef = sb("out_coef", [P, 1], F32)
        wg_int = sb("wg_int", [P, HC, D], I32)
        wu_int = sb("wu_int", [P, HC, D], I32)
        wd_int = sb("wd_int", [P, DC, HID], I32)
        wg16 = sb("wg16", [P, HC, D], F16)
        wu16 = sb("wu16", [P, HC, D], F16)
        wd16 = sb("wd16", [P, DC, HID], F16)
        wg_T = sb("wg_T", [P, DC, HID], F16)
        wu_T = sb("wu_T", [P, DC, HID], F16)
        wd_T = sb("wd_T", [P, HC, D], F16)

        stats = sb("stats", [P, 2, TILES, 6], F32)
        mean_sum = sb("mean_sum", [P, 2, TILES], F32)
        mean_gap = sb("mean_gap", [P, 2, TILES], F32)
        sq_sum = sb("sq_sum", [P, 2, TILES], F32)
        mean = sb("mean", [P, 2, TILES], F32)
        gap_sq = sb("gap_sq", [P, 2, TILES], F32)
        var = sb("var", [P, 2, TILES], F32)
        var_eps = sb("var_eps", [P, 2, TILES], F32)
        rsqrt = sb("rsqrt", [P, NEWTON + 1, 2, TILES], F32)
        rsqrt_sq = sb("rsqrt_sq", [P, NEWTON, 2, TILES], F32)
        rsqrt_res = sb("rsqrt_res", [P, NEWTON, 2, TILES], F32)
        xn1 = sb("xn1", [P, TILES, D], F32)
        xn2 = sb("xn2", [P, TILES, D], F32)
        xn1_T = sb("xn1_T", [P, DC, BLOCK], F32)
        scores = sb("scores", [P, TILES, M], F32)
        neg_max = sb("neg_max", [P, TILES], F32)
        probs = sb("probs", [P, TILES, M], F32)
        probs_hl = sb("probs_hl", [P, TILES, 2, M], F32R)
        prob_sum = sb("prob_sum", [P, TILES], F32)
        prob_rcp = sb("prob_rcp", [P, TILES], F32)
        attn_coef = sb("attn_coef", [P, TILES], F32)
        probs_T = sb("probs_T", [2 * M, BLOCK], F32R)
        xhi = sb("xhi", [P, DC, BLOCK], F16)
        xlo = sb("xlo", [P, DC, BLOCK], F16)
        silu = sb("silu", [P, 2, BLOCK], F32)
        h32 = sb("h32", [P, HC, BLOCK], F32)
        hhi = sb("hhi", [P, HC, BLOCK], F16)
        hlo = sb("hlo", [P, HC, BLOCK], F16)
        w_abs = sb("w_abs", [P, 3], F32)
        w_max = sb("w_max", [P, 1], F32)
        w_wide = sb("w_wide", [P, 1], F32)
        ones_col = sb("ones_col", [P, 1], F32)
        wide_flag = sb("wide_flag", [1, 1], I32)
        wgF_T = sb("wgF_T", [P, DC, HID], F32)
        wuF_T = sb("wuF_T", [P, DC, HID], F32)
        wdF_T = sb("wdF_T", [P, HC, D], F32)
        y_sb = sb("y_sb", [P, 2, TILES * D], F32)

        gate_ps = [psum("gate_ps0"), psum("gate_ps1")]
        up_ps = [psum("up_ps0"), psum("up_ps1")]
        out_ps = [psum("out_ps0"), psum("out_ps1")]
        att_ps = [psum("att_ps0"), psum("att_ps1")]

        x_in = [sem("x_in0"), sem("x_in1")]
        W_in, ctx_in, ctxm_in, small_in = sem("W_in"), sem("ctx_in"), sem("ctxm_in"), sem("small_in")
        wg_in, wu_in, wd_in = sem("wg_in"), sem("wu_in"), sem("wd_in")
        y_free = [sem("y_free0"), sem("y_free1")]
        ident_set, b_rep_set = sem("ident_set"), sem("b_rep_set")
        setup_T, setup_T_act, setup_T_dve = sem("setup_T"), sem("setup_T_act"), sem("setup_T_dve")
        eo_done, eo_copied = sem("eo_done"), sem("eo_copied")
        key_done, key_copied = sem("key_done"), sem("key_copied")
        bdot_done, bdot_copied = sem("bdot_done"), sem("bdot_copied")
        tanh_done, coef_done = sem("tanh_done"), sem("coef_done")
        w16_ready = sem("w16_ready")
        wT_done = sem("wT_done")
        gate_free = sem("gate_free")
        up_free = sem("up_free")
        out_free = sem("out_free")
        bn_done, ln_math, xn_ready = sem("bn_done"), sem("ln_math"), sem("xn_ready")
        t1_done, t1_copied = sem("t1_done"), sem("t1_copied")
        s_done, s_added, max_ready = sem("s_done"), sem("s_added"), sem("max_ready")
        probs_ready = sem("probs_ready")
        phi_ready, plo_ready = sem("phi_ready"), sem("plo_ready")
        ctx_split = sem("ctx_split")
        rcp_done, acoef_ready = sem("rcp_done"), sem("acoef_ready")
        pt_done, pt_copied = sem("pt_done"), sem("pt_copied")
        pv_done, x1_ready = sem("pv_done"), sem("x1_ready")
        t2_done, xhi_ready, xlo_ready = sem("t2_done"), sem("xhi_ready"), sem("xlo_ready")
        gu_done = sem("gu_done")
        hhi_ready, hlo_ready = sem("hhi_ready"), sem("hlo_ready")
        down_done = sem("down_done")
        abs_done, wide_col, wide_sum, flag_set = sem("abs_done"), sem("wide_col"), sem("wide_sum"), sem("flag_set")
        wf_ready, wfT_done, wfT_copied = sem("wf_ready"), sem("wfT_done"), sem("wfT_copied")
        gen_bn, gen_xn, gen_xT, gen_xT_copied = sem("gen_bn"), sem("gen_xn"), sem("gen_xT"), sem("gen_xT_copied")
        gen_gu, gen_silu, gen_h, gen_down, gen_y = sem("gen_gu"), sem("gen_silu"), sem("gen_h"), sem("gen_down"), sem("gen_y")

        def x_tile(k, j):
            return xs[:, bass.ds(k * (TILES * D) + j * D, D)]

        gate_up_banks = [gate_ps[0], gate_ps[1], up_ps[0]]
        h32_rows = h32[:].rearrange("p c n -> p (c n)")[:, 0:HC * D]

        def general_groups():
            flat = "p a b -> p (a b)"
            return ((wg_int[:].rearrange(flat), wgF_T[:].rearrange(flat), [(c * D + d * P) for d in range(DC) for c in range(HC)]),
                    (wu_int[:].rearrange(flat), wuF_T[:].rearrange(flat), [(c * D + d * P) for d in range(DC) for c in range(HC)]),
                    (wd_int[:].rearrange(flat), wdF_T[:].rearrange(flat), [(d * HID + c * P) for c in range(HC) for d in range(DC)]))

        FAST_STORES = 16 * (BLOCKS // 2 + 1)
        FAST_Y = 4 * BLOCKS + 2

        def weights_are_wide(eng):
            eng.wait_ge(flag_set, 1)
            return eng.value_load(wide_flag[0:1, 0:1], min_val=0, max_val=P) > 0

        block = stack.enter_context(nc.Block())

        @block.sync
        def _(sp):
            def load_x(k, par):
                sp.dma_start(xs[:, bass.ds(k * (TILES * D), TILES * D)], x_v[bass.ds(k, 1)].rearrange("k p f -> (k p) f")).then_inc(x_in[par], 16)

            def store_y(k, par):
                sp.wait_ge(out_free, 4 * k + 6)
                sp.dma_start(out_v[bass.ds(k, 1)].rearrange("k p f -> (k p) f"), y_sb[:, par]).then_inc(y_free[par], 16)

            sp.dma_start(ctx_nat[:], ctx.rearrange("b m d -> (b m) d").rearrange("(c p) d -> p c d", p=P)).then_inc(ctx_in, 16)
            sp.dma_start(W_nat[:], W.rearrange("(c p) d -> p c d", p=P)).then_inc(W_in, 16)
            load_x(0, 0)
            for half in range(2):
                sp.dma_start(ctx_m[half * M:(half + 1) * M].rearrange("m (b d) -> m b d", b=B),
                             ctx.rearrange("b m d -> m b d")).then_inc(ctxm_in, 16)
            load_x(1, 1)

            def two_steps(i, last):
                for par in range(2):
                    if not last:
                        sp.wait_ge(x_in[par], 16 * i + 16)
                        load_x(2 * i + par + 2, par)
                    store_y(2 * i + par, par)

            with sp.Fori(0, BLOCKS // 2 - 1) as i:
                two_steps(i, False)
            two_steps(BLOCKS // 2 - 1, True)
            for par in range(2):
                sp.wait_ge(y_free[par], FAST_STORES)
            with sp.If(weights_are_wide(sp)):
                with sp.Fori(0, BLOCKS) as k:
                    sp.wait_ge(gen_y, 4 * k + 4)
                    sp.dma_start(out_v[bass.ds(k, 1)].rearrange("k p f -> (k p) f"), y_sb[:, 0]).then_inc(y_free[0], 16)
                sp.wait_ge(y_free[0], FAST_STORES + 16 * BLOCKS)

        @block.scalar
        def _(act):
            act.dma_start(b_col[:], b.rearrange("(c p) -> p c", p=P), allow_slow_non_contiguous=True).then_inc(small_in, 16)
            act.dma_start(g_raw[:, 0:1], g_xattn.partition_broadcast(P)).then_inc(small_in, 16)
            act.dma_start(g_raw[:, 1:2], g_ffn.partition_broadcast(P)).then_inc(small_in, 16)
            act.dma_start(wg_int[:], w_gate.rearrange("(c p) d -> p c d", p=P)).then_inc(wg_in, 16)
            act.dma_start(wu_int[:], w_up.rearrange("(c p) d -> p c d", p=P)).then_inc(wu_in, 16)
            act.dma_start(wd_int[:], w_down.rearrange("(c p) h -> p c h", p=P)).then_inc(wd_in, 16)

            def copy_t1(a):
                for c in range(DC):
                    act.wait_ge(t1_done, 2 * a + c + 1)
                    nc.scalar.copy(xn1_T[:, c], att_ps[c][:]).then_inc(t1_copied, 1)

            def exp_scores(a):
                act.wait_ge(max_ready, a + 1)
                for j in range(TILES):
                    last = nc.scalar.activation(probs[:, j], scores[:, j], ACT.Exp, bias=neg_max[:, j:j + 1],
                                                accum_out=prob_sum[:, j:j + 1])
                last.then_inc(probs_ready, 1)

            def copy_pt(a):
                act.wait_ge(pt_done, a + 1)
                nc.scalar.copy(probs_T[:], att_ps[1][:]).then_inc(pt_copied, 1)

            def x_high(a):
                for c in range(DC):
                    act.wait_ge(t2_done, 2 * a + c + 1)
                    nc.scalar.mul(xhi[:, c], att_ps[c][:], LN_SCALE).then_inc(xhi_ready, 1)

            def silu_gate(k, c):
                act.wait_ge(gu_done, 6 * k + c + 1)
                nc.scalar.activation(silu[:, c % 2], gate_ps[c % 2][:], ACT.Silu,
                                     scale=1.0 / (LN_SCALE * QUANT)).then_inc(gate_free, 1)

            def h_high(k, c):
                act.wait_ge(up_free, 6 * k + c + 3)
                nc.scalar.copy(hhi[:, c], h32[:, c]).then_inc(hhi_ready, 1)

            act.wait_ge(small_in, 48)
            nc.scalar.activation(g_tanh[:], g_raw[:], ACT.Tanh).then_inc(tanh_done, 1)
            act.wait_ge(setup_T, 1)
            nc.scalar.copy(W_T[:].rearrange("p c e -> p (c e)"), att_ps[0][:]).then_inc(setup_T_act, 1)
            act.wait_ge(eo_done, 1)
            for c in range(DC):
                last = nc.scalar.activation(eo_T[:, c], out_ps[0][:, c * ROWS:(c + 1) * ROWS], ACT.Identity,
                                            bias=b_col[:, c:c + 1])
            last.then_inc(eo_copied, 1)
            act.wait_ge(bdot_done, 1)
            nc.scalar.copy(b_dot[:], out_ps[0][:, 0:ROWS]).then_inc(bdot_copied, 1)
            copy_t1(0)
            for c in range(DC):
                act.wait_ge(wT_done, c + 1)
                nc.scalar.copy(wg_T[:, c].bitcast(F32), gate_ps[c][:, 0:HID // 2]).then_inc(gate_free, 1)
            exp_scores(0)
            copy_pt(0)
            x_high(0)

            def step(k, attention):
                silu_gate(k, 0)
                if attention:
                    copy_t1(k + 1)
                silu_gate(k, 1)
                h_high(k, 0)
                silu_gate(k, 2)
                h_high(k, 1)
                if attention:
                    exp_scores(k + 1)
                silu_gate(k, 3)
                h_high(k, 2)
                if attention:
                    copy_pt(k + 1)
                silu_gate(k, 4)
                h_high(k, 3)
                silu_gate(k, 5)
                h_high(k, 4)
                h_high(k, 5)
                if attention:
                    x_high(k + 1)

            with act.Fori(0, BLOCKS // 2 - 1) as i:
                step(2 * i, True)
                step(2 * i + 1, True)
            step(BLOCKS - 2, True)
            step(BLOCKS - 1, False)

            with act.If(weights_are_wide(act)):
                act.wait_ge(out_free, FAST_Y)
                with act.Fori(0, BLOCKS) as k:
                    for j in range(TILES):
                        act.wait_ge(gen_gu, 4 * k + j + 1)
                        for g, (bank, n) in enumerate(zip(gate_ps, (512, HID - 512))):
                            last = nc.scalar.activation(silu[:].rearrange("p a n -> p (a n)")[:, g * 512:g * 512 + n],
                                                        bank[:, 0:n], ACT.Silu)
                        last.then_inc(gen_silu, 1)

        @block.gpsimd
        def _(pool):
            nc.gpsimd.memset(ident[:], 0.0).then_inc(ident_set, 1)
            pool.wait_ge(ident_set, 1)
            nc.gpsimd.affine_select(out=ident[:], in_=ident[:], compare_op=ALU.not_equal, fill=1.0, base=0,
                                    pattern=[[-1, P]], channel_multiplier=1).then_inc(ident_set, 1)
            pool.wait_ge(ident_set, 2)
            nc.gpsimd.tensor_copy(ident16[:], ident[:]).then_inc(ident_set, 1)

            def h_low(k, c):
                pool.wait_ge(hhi_ready, 6 * k + c + 1)
                nc.gpsimd.tensor_tensor(hlo[:, c], h32[:, c], hhi[:, c], ALU.subtract).then_inc(hlo_ready, 1)

            pool.wait_ge(ctxm_in, 32)
            nc.gpsimd.tensor_copy(ctx_hi[:], ctx_m[:]).then_inc(ctx_split, 1)
            pool.wait_ge(ctx_split, 1)
            nc.gpsimd.tensor_tensor(ctx_lo[:], ctx_m[:], ctx_hi[:].bitcast(F32), ALU.subtract).then_inc(ctx_split, 1)

            with pool.Fori(0, BLOCKS) as k:
                for c in range(HC):
                    h_low(k, c)

        @block.vector
        def _(dve):
            def norm_stats(k, w):
                for j in range(TILES):
                    last = nc.vector.bn_stats(stats[:, w, j], x_tile(k, j))
                last.then_inc(bn_done, 1)

            def norm_factors(m, half, stats_needed, stats_sem=bn_done):
                n = LN_OPS * m
                even, odd = stats[:, half, :, 0:3], stats[:, half, :, 3:6]
                v = nc.vector
                dve.wait_ge(stats_sem, stats_needed)
                v.tensor_tensor(mean_sum[:, half], even[:, :, :, 1], odd[:, :, :, 1], ALU.add).then_inc(ln_math, 1)
                v.tensor_tensor(mean_gap[:, half], even[:, :, :, 1], odd[:, :, :, 1], ALU.subtract).then_inc(ln_math, 1)
                v.tensor_tensor(sq_sum[:, half], even[:, :, :, 2], odd[:, :, :, 2], ALU.add).then_inc(ln_math, 1)
                dve.wait_ge(ln_math, n + 2)
                v.scalar_tensor_tensor(out=gap_sq[:, half], in0=mean_gap[:, half], scalar=0.25, in1=mean_gap[:, half],
                                       op0=ALU.mult, op1=ALU.mult).then_inc(ln_math, 1)
                v.tensor_scalar(mean[:, half], mean_sum[:, half], 0.5, None, ALU.mult).then_inc(ln_math, 1)
                dve.wait_ge(ln_math, n + 4)
                v.scalar_tensor_tensor(out=var[:, half], in0=sq_sum[:, half], scalar=1.0 / D, in1=gap_sq[:, half],
                                       op0=ALU.mult, op1=ALU.add).then_inc(ln_math, 1)
                dve.wait_ge(ln_math, n + 6)
                v.tensor_scalar(var_eps[:, half], var[:, half], EPS, None, ALU.add).then_inc(ln_math, 1)
                dve.wait_ge(ln_math, n + 7)
                v.tensor_scalar(rsqrt[:, 0, half].bitcast(I32), var_eps[:, half].bitcast(I32), -0.5, RSQRT_MAGIC,
                                ALU.mult, ALU.add).then_inc(ln_math, 1)
                for t in range(NEWTON):
                    y = rsqrt[:, t, half]
                    dve.wait_ge(ln_math, n + 8 + 3 * t)
                    v.tensor_tensor(rsqrt_sq[:, t, half], y, y, ALU.mult).then_inc(ln_math, 1)
                    dve.wait_ge(ln_math, n + 9 + 3 * t)
                    v.scalar_tensor_tensor(out=rsqrt_res[:, t, half], in0=rsqrt_sq[:, t, half], scalar=-0.5,
                                           in1=var_eps[:, half], op0=ALU.mult, op1=ALU.mult).then_inc(ln_math, 1)
                    dve.wait_ge(ln_math, n + 10 + 3 * t)
                    v.scalar_tensor_tensor(out=rsqrt[:, t + 1, half], in0=rsqrt_res[:, t, half], scalar=1.5, in1=y,
                                           op0=ALU.add, op1=ALU.mult).then_inc(ln_math, 1)

            def normalise(k, dst, m, w):
                dve.wait_ge(ln_math, LN_OPS * (m + 1))
                for j in range(TILES):
                    last = nc.vector.tensor_scalar(dst[:, j], x_tile(k, j), mean[:, w, j:j + 1],
                                                   rsqrt[:, NEWTON, w, j:j + 1], ALU.subtract, ALU.mult)
                last.then_inc(xn_ready, 1)

            def row_max(a, batch):
                dve.wait_ge(s_done, a + 1)
                bd = b_dot[:, bass.ds(batch * M, M)].unsqueeze(1).broadcast_to([P, TILES, M])
                nc.vector.tensor_tensor(scores[:], att_ps[0][:, 0:TILES * M].rearrange("p (j m) -> p j m", j=TILES),
                                        bd, ALU.add).then_inc(s_added, 1)
                dve.wait_ge(s_added, a + 1)
                nc.vector.tensor_reduce(neg_max[:], scores[:], AX.X, ALU.max, negate=True).then_inc(max_ready, 1)

            def split_probs(a):
                dve.wait_ge(probs_ready, a + 1)
                nc.vector.tensor_copy(probs_hl[:, :, 0], probs[:]).then_inc(phi_ready, 1)
                dve.wait_ge(phi_ready, a + 1)
                nc.vector.tensor_tensor(probs_hl[:, :, 1], probs[:], probs_hl[:, :, 0].bitcast(F32),
                                        ALU.subtract).then_inc(plo_ready, 1)
                nc.vector.reciprocal(prob_rcp[:], prob_sum[:]).then_inc(rcp_done, 1)
                dve.wait_ge(rcp_done, a + 1)
                nc.vector.tensor_scalar(attn_coef[:], prob_rcp[:], g_tanh[:, 0:1], None, ALU.mult).then_inc(acoef_ready, 1)

            def add_attention(a):
                dve.wait_ge(acoef_ready, a + 1)
                for j in range(TILES):
                    if j % 2 == 0:
                        dve.wait_ge(pv_done, 2 * a + j // 2 + 1)
                    last = nc.vector.scalar_tensor_tensor(out=x_tile(a, j), in0=att_ps[j // 2][:, (j % 2) * D:(j % 2 + 1) * D],
                                                          scalar=attn_coef[:, j:j + 1], in1=x_tile(a, j),
                                                          op0=ALU.mult, op1=ALU.add)
                last.then_inc(x1_ready, 1)

            def x_low(a):
                for c in range(DC):
                    dve.wait_ge(xhi_ready, 2 * a + c + 1)
                    nc.vector.scalar_tensor_tensor(out=xlo[:, c], in0=att_ps[c][:], scalar=LN_SCALE, in1=xhi[:, c],
                                                   op0=ALU.mult, op1=ALU.subtract).then_inc(xlo_ready, 1)

            def h_of(k, c):
                dve.wait_ge(gate_free, 6 * k + c + 3)
                nc.vector.scalar_tensor_tensor(out=h32[:, c], in0=up_ps[c % 2][:], scalar=H_SCALE / (LN_SCALE * QUANT),
                                               in1=silu[:, c % 2], op0=ALU.mult, op1=ALU.mult).then_inc(up_free, 1)

            def add_ffn(k, i, par):
                dve.wait_ge(y_free[par], 16 * i + 16)
                for j in range(TILES):
                    if j % 2 == 0:
                        dve.wait_ge(down_done, 2 * k + j // 2 + 1)
                    nc.vector.scalar_tensor_tensor(out=y_sb[:, par, j * D:(j + 1) * D],
                                                   in0=out_ps[j // 2][:, (j % 2) * D:(j % 2 + 1) * D],
                                                   scalar=out_coef[:, 0:1], in1=x_tile(k, j),
                                                   op0=ALU.mult, op1=ALU.add).then_inc(out_free, 1)

            dve.wait_ge(setup_T, 2)
            nc.vector.tensor_copy(ctx_T[:].rearrange("p c r -> p (c r)"), att_ps[1][:]).then_inc(setup_T_dve, 1)
            dve.wait_ge(small_in, 48)
            for c in range(DC):
                nc.vector.tensor_copy(b_rep[:, c], b_col[:, c:c + 1].broadcast_to([P, P])).then_inc(b_rep_set, 1)
            dve.wait_ge(tanh_done, 1)
            nc.vector.tensor_scalar(out_coef[:], g_tanh[:, 1:2], 1.0 / (H_SCALE * QUANT), None, ALU.mult).then_inc(coef_done, 1)
            nc.vector.memset(ones_col[:], 1.0).then_inc(coef_done, 1)
            for half in range(2):
                nc.vector.memset(y_sb[:, half, 0:1], 0.0).then_inc(y_free[half], 16)
            dve.wait_ge(x_in[0], 16)
            norm_stats(0, 0)
            norm_factors(0, slice(0, 1), 1)
            normalise(0, xn1, 0, 0)
            dve.wait_ge(key_done, 1)
            nc.vector.tensor_copy(key_T[:].rearrange("p c r -> p (c r)"), out_ps[1][:]).then_inc(key_copied, 1)
            for w_in, w16, w_int in ((wg_in, wg16, wg_int), (wu_in, wu16, wu_int), (wd_in, wd16, wd_int)):
                dve.wait_ge(w_in, 16)
                nc.vector.tensor_copy(w16[:], w_int[:]).then_inc(w16_ready, 1)
            dve.wait_ge(bdot_copied, 1)
            row_max(0, 0)
            for c in range(DC):
                dve.wait_ge(wT_done, 2 + c + 1)
                nc.vector.tensor_copy(wu_T[:, c].bitcast(F32), up_ps[c][:, 0:HID // 2]).then_inc(up_free, 1)
            for c in range(2):
                dve.wait_ge(wT_done, 4 + c + 1)
                nc.vector.tensor_copy(wd_T[:, c * (HC // 2):(c + 1) * (HC // 2)].rearrange("p c d -> p (c d)").bitcast(F32),
                                      out_ps[c][:, 0:HID // 2]).then_inc(out_free, 1)
            split_probs(0)
            add_attention(0)
            dve.wait_ge(x_in[1], 16)
            norm_stats(1, 0)
            dve.wait_ge(x1_ready, 1)
            norm_stats(0, 1)
            norm_factors(1, slice(0, 2), 3)
            normalise(0, xn2, 1, 1)
            x_low(0)
            normalise(1, xn1, 1, 0)
            dve.wait_ge(coef_done, 2)

            def step(k, i, par, batch, attention, prefetch):
                h_of(k, 0)
                h_of(k, 1)
                if attention:
                    row_max(k + 1, batch)
                if prefetch:
                    dve.wait_ge(x_in[par], 16 * i + 32)
                h_of(k, 2)
                if prefetch:
                    norm_stats(k + 2, 0)
                if attention:
                    split_probs(k + 1)
                h_of(k, 3)
                h_of(k, 4)
                if attention:
                    add_attention(k + 1)
                    dve.wait_ge(x1_ready, k + 2)
                h_of(k, 5)
                if not attention:
                    for n, w_int in enumerate((wg_int, wu_int, wd_int)):
                        last = nc.vector.tensor_reduce(w_abs[:, n:n + 1], w_int[:], AX.XY, ALU.max, apply_absolute_value=True)
                    last.then_inc(abs_done, 1)
                    dve.wait_ge(abs_done, 1)
                    nc.vector.tensor_reduce(w_max[:], w_abs[:], AX.X, ALU.max).then_inc(abs_done, 1)
                    dve.wait_ge(abs_done, 2)
                    nc.vector.tensor_scalar(w_wide[:], w_max[:], QUANT, None, ALU.is_gt).then_inc(wide_col, 1)
                    dve.wait_ge(wide_sum, 1)
                    nc.vector.tensor_copy(wide_flag[:], att_ps[0][0:1, 0:1]).then_inc(flag_set, 1)
                if attention:
                    norm_stats(k + 1, 1)
                    norm_factors(k + 2, slice(0 if prefetch else 1, 2), 2 * k + 5 if prefetch else 2 * k + 4)
                    normalise(k + 1, xn2, k + 2, 1)
                    x_low(k + 1)
                if prefetch:
                    normalise(k + 2, xn1, k + 2, 0)
                add_ffn(k, i, par)

            with dve.Fori(0, BLOCKS // 2 - 1) as i:
                step(2 * i, i, 0, i, True, True)
                step(2 * i + 1, i, 1, i + 1, True, True)
            last = BLOCKS // 2 - 1
            step(2 * last, last, 0, last, True, False)
            step(2 * last + 1, last, 1, None, False, False)

            with dve.If(weights_are_wide(dve)):
                dve.wait_ge(out_free, FAST_Y)
                groups = general_groups()
                for n, (w_int, _, _) in enumerate(groups):
                    if n:
                        dve.wait_ge(wfT_done, 3 * n)
                    nc.vector.tensor_scalar(h32_rows, w_int, 1.0 / QUANT, None, ALU.mult).then_inc(wf_ready, 1)
                    for g in range(3):
                        dve.wait_ge(wfT_done, 3 * n + g + 1)
                        nc.vector.tensor_copy(groups[n][1][:, g * 512:(g + 1) * 512], gate_up_banks[g][:]).then_inc(wfT_copied, 1)

                def general_tile(k, j):
                    t = 4 * k + j
                    nc.vector.bn_stats(stats[:, 0, 0], x_tile(k, j)).then_inc(gen_bn, 1)
                    norm_factors(BLOCKS + 1 + t, slice(0, 1), t + 1, gen_bn)
                    dve.wait_ge(ln_math, LN_OPS * (BLOCKS + 2 + t))
                    nc.vector.tensor_scalar(xn1[:, 0], x_tile(k, j), mean[:, 0, 0:1], rsqrt[:, NEWTON, 0, 0:1],
                                            ALU.subtract, ALU.mult).then_inc(gen_xn, 1)
                    dve.wait_ge(gen_xT, t + 1)
                    nc.vector.tensor_copy(xn1_T[:, 0, 0:D], att_ps[0][:, 0:D]).then_inc(gen_xT_copied, 1)
                    dve.wait_ge(gen_silu, t + 1)
                    for g, (bank, n) in enumerate(zip(up_ps, (512, HID - 512))):
                        last = nc.vector.tensor_tensor(h32[:].rearrange("p c n -> p (c n)")[:, g * 512:g * 512 + n], bank[:, 0:n],
                                                       silu[:].rearrange("p a n -> p (a n)")[:, g * 512:g * 512 + n], ALU.mult)
                    last.then_inc(gen_h, 1)
                    if j == 0:
                        dve.wait_ge(y_free[0], 16 * k + FAST_STORES)
                    dve.wait_ge(gen_down, t + 1)
                    nc.vector.scalar_tensor_tensor(out=y_sb[:, 0, j * D:(j + 1) * D], in0=out_ps[0][:, 0:D],
                                                   scalar=g_tanh[:, 1:2], in1=x_tile(k, j), op0=ALU.mult, op1=ALU.add).then_inc(gen_y, 1)

                with dve.Fori(0, BLOCKS) as k:
                    for j in range(TILES):
                        general_tile(k, j)

        @block.tensor
        def _(pe):
            mm = nc.tensor.matmul

            def t1(a):
                pe.wait_ge(xn_ready, 2 * a + 1)
                for c in range(DC):
                    for j in range(TILES):
                        last = nc.tensor.transpose(att_ps[c][:, j * P:(j + 1) * P], xn1[:, j, c * P:(c + 1) * P], ident[:])
                    last.then_inc(t1_done, 1)

            def score(a, batch):
                pe.wait_ge(t1_copied, 2 * a + 2)
                for j in range(TILES):
                    for c in range(DC):
                        last = mm(att_ps[0][:, j * M:(j + 1) * M], xn1_T[:, c, j * P:(j + 1) * P],
                                  key_T[:, c, bass.ds(batch * M, M)], start=(c == 0), stop=(c == DC - 1))
                last.then_inc(s_done, 1)

            def transpose_probs(a):
                pe.wait_ge(plo_ready, a + 1)
                for j in range(TILES):
                    last = nc.tensor.transpose(att_ps[1][:, j * P:(j + 1) * P],
                                               probs_hl[:, j].rearrange("p h m -> p (h m)").bitcast(F32), ident[:])
                last.then_inc(pt_done, 1)

            def attend(a, batch):
                pe.wait_ge(pt_copied, a + 1)
                for j in range(TILES):
                    for n, c_half in enumerate((ctx_hi, ctx_lo)):
                        last = mm(att_ps[j // 2][:, (j % 2) * D:(j % 2 + 1) * D], probs_T[:, j * P:(j + 1) * P],
                                  c_half[:, bass.ds(batch * D, D)], start=(n == 0), stop=(n == 1))
                    if j % 2 == 1:
                        last.then_inc(pv_done, 1)

            def t2(a):
                pe.wait_ge(xn_ready, 2 * a + 2)
                for c in range(DC):
                    for j in range(TILES):
                        last = nc.tensor.transpose(att_ps[c][:, j * P:(j + 1) * P], xn2[:, j, c * P:(c + 1) * P], ident[:])
                    last.then_inc(t2_done, 1)

            def gate_up(k, c):
                if c == 0:
                    pe.wait_ge(xhi_ready, 2 * k + 2)
                pe.wait_ge(gate_free, 6 * k + c + 1)
                pe.wait_ge(up_free, 6 * k + c + 1)
                for w_T, bank in ((wg_T, gate_ps[c % 2]), (wu_T, up_ps[c % 2])):
                    for n, half in enumerate((xhi, xlo)):
                        if c == 0 and n == 1 and w_T is wg_T:
                            pe.wait_ge(xlo_ready, 2 * k + 2)
                        for d in range(DC):
                            last = mm(bank[:], w_T[:, d, c * P:(c + 1) * P], half[:, d],
                                      start=(n == 0 and d == 0), stop=(n == 1 and d == DC - 1))
                last.then_inc(gu_done, 1)

            def down(k, c):
                if c == 0:
                    pe.wait_ge(out_free, 4 * k + 2)
                pe.wait_ge(hlo_ready, 6 * k + c + 1)
                for j in range(TILES):
                    for n, half in enumerate((hhi, hlo)):
                        last = mm(out_ps[j // 2][:, (j % 2) * D:(j % 2 + 1) * D], half[:, c, j * P:(j + 1) * P], wd_T[:, c],
                                  start=(c == 0 and n == 0 and j % 2 == 0), stop=(c == HC - 1 and n == 1),
                                  skip_group_check=True)
                    if c == HC - 1 and j % 2 == 1:
                        last.then_inc(down_done, 1)

            pe.wait_ge(ident_set, 3)
            for srcs, ready, bank in ((W_nat, W_in, 0), (ctx_nat, ctx_in, 1)):
                pe.wait_ge(ready, 16)
                for d in range(DC):
                    for r in range(2):
                        o = d * 2 * P + r * P
                        last = nc.tensor.transpose(att_ps[bank][:, o:o + P], srcs[:, r, d * P:(d + 1) * P], ident[:])
                last.then_inc(setup_T, 1)
            pe.wait_ge(setup_T_act, 1)
            pe.wait_ge(setup_T_dve, 1)
            for e in range(DC):
                for d in range(DC):
                    last = mm(out_ps[0][:, e * ROWS:(e + 1) * ROWS], W_T[:, d, e * P:(e + 1) * P], ctx_T[:, d],
                              start=(d == 0), stop=(d == DC - 1))
            last.then_inc(eo_done, 1)
            t1(0)
            pe.wait_ge(eo_copied, 1)
            for d in range(DC):
                for e in range(DC):
                    last = mm(out_ps[1][:, d * ROWS:(d + 1) * ROWS], W_nat[:, e, d * P:(d + 1) * P], eo_T[:, e],
                              start=(e == 0), stop=(e == DC - 1))
            last.then_inc(key_done, 1)
            pe.wait_ge(b_rep_set, 2)
            for e in range(DC):
                last = mm(out_ps[0][:, 0:ROWS], b_rep[:, e], eo_T[:, e], start=(e == 0), stop=(e == DC - 1))
            last.then_inc(bdot_done, 1)
            pe.wait_ge(key_copied, 1)
            score(0, 0)

            def transpose_gate_or_up(w16, banks, n):
                pe.wait_ge(w16_ready, n)
                for d in range(DC):
                    o = banks[d][:].bitcast(F16)
                    for c in range(HC):
                        last = nc.tensor.transpose(o[:, c * P:(c + 1) * P], w16[:, c, d * P:(d + 1) * P], ident16[:])
                    last.then_inc(wT_done, 1)

            transpose_gate_or_up(wg16, gate_ps, 1)
            transpose_gate_or_up(wu16, up_ps, 2)
            pe.wait_ge(bdot_copied, 1)
            pe.wait_ge(w16_ready, 3)
            for g in range(2):
                o = out_ps[g][:].bitcast(F16)
                for c in range(HC // 2):
                    for d in range(DC):
                        h0 = (g * (HC // 2) + c) * P
                        last = nc.tensor.transpose(o[:, (c * DC + d) * P:(c * DC + d + 1) * P], wd16[:, d, h0:h0 + P], ident16[:])
                last.then_inc(wT_done, 1)
            transpose_probs(0)
            pe.wait_ge(ctx_split, 2)
            attend(0, 0)
            t2(0)

            def step(k, batch, attention):
                gate_up(k, 0)
                if attention:
                    t1(k + 1)
                gate_up(k, 1)
                if attention:
                    score(k + 1, batch)
                gate_up(k, 2)
                gate_up(k, 3)
                if attention:
                    transpose_probs(k + 1)
                gate_up(k, 4)
                if attention:
                    attend(k + 1, batch)
                gate_up(k, 5)
                if not attention:
                    pe.wait_ge(wide_col, 1)
                    pe.wait_ge(coef_done, 2)
                    mm(att_ps[0][0:1, 0:1], w_wide[:], ones_col[:], start=True, stop=True).then_inc(wide_sum, 1)
                for c in range(HC - 1):
                    down(k, c)
                if attention:
                    t2(k + 1)
                down(k, HC - 1)

            with pe.Fori(0, BLOCKS // 2 - 1) as i:
                step(2 * i, i, True)
                step(2 * i + 1, i + 1, True)
            step(BLOCKS - 2, B - 1, True)
            step(BLOCKS - 1, None, False)

            with pe.If(weights_are_wide(pe)):
                pe.wait_ge(out_free, FAST_Y)
                for n, (_, _, blocks) in enumerate(general_groups()):
                    pe.wait_ge(wf_ready, n + 1)
                    for g in range(3):
                        if n:
                            pe.wait_ge(wfT_copied, 3 * (n - 1) + g + 1)
                        for q in range(4):
                            at = blocks[4 * g + q]
                            last = nc.tensor.transpose(gate_up_banks[g][:, q * P:(q + 1) * P], h32_rows[:, at:at + P], ident[:])
                        last.then_inc(wfT_done, 1)
                pe.wait_ge(wfT_copied, 9)
                with pe.Fori(0, BLOCKS) as k:
                    for j in range(TILES):
                        t = 4 * k + j
                        pe.wait_ge(gen_xn, t + 1)
                        for d in range(DC):
                            last = nc.tensor.transpose(att_ps[0][:, d * P:(d + 1) * P], xn1[:, 0, d * P:(d + 1) * P], ident[:])
                        last.then_inc(gen_xT, 1)
                        pe.wait_ge(gen_xT_copied, t + 1)
                        for w_T, banks in ((wgF_T, gate_ps), (wuF_T, up_ps)):
                            for c in range(HC):
                                for d in range(DC):
                                    last = mm(banks[c // 4][:, c % 4 * P:(c % 4 + 1) * P], w_T[:, d, c * P:(c + 1) * P],
                                              xn1_T[:, 0, d * P:(d + 1) * P], start=(d == 0), stop=(d == DC - 1))
                        last.then_inc(gen_gu, 1)
                        pe.wait_ge(gen_h, t + 1)
                        for c in range(HC):
                            last = mm(out_ps[0][:, 0:D], h32[:].rearrange("p c n -> p (c n)")[:, c * P:(c + 1) * P], wdF_T[:, c],
                                      start=(c == 0), stop=(c == HC - 1))
                        last.then_inc(gen_down, 1)


_INS = ["x", "ctx_1024", "g_xattn", "g_ffn", "L0_xattn_W", "L0_xattn_b", "L0_ffn_w_gate", "L0_ffn_w_up", "L0_ffn_w_down"]


def kernel(**inputs):
    import numpy as np
    import concourse.bacc as bacc
    from concourse import mybir as mb
    from concourse.bass_utils import run_bass_kernel_spmd as run

    nc = bacc.Bacc("TRN2", target_bir_lowering=False, num_devices=1)
    arrays, args = {}, []
    for name in _INS:
        a = np.ascontiguousarray(inputs[name])
        arrays[f"in_{name}"] = a
        args.append(nc.dram_tensor(f"in_{name}", a.shape, mb.dt.from_np(a.dtype), kind="ExternalInput").ap())
    x = arrays["in_x"]
    o = nc.dram_tensor("out_y", x.shape, mb.dt.float32, kind="ExternalOutput").ap()
    gated_cross_attention_and_ffn(nc, *args, o)
    r = run(nc, [arrays], core_ids=[0])
    return r.results[0]["out_y"]
```

```python
from contextlib import ExitStack

import concourse.bass as bass
from concourse import mybir

F32 = mybir.dt.float32
F32R = mybir.dt.float32r
F16 = mybir.dt.float16
I32 = mybir.dt.int32
ALU = mybir.AluOpType
ACT = mybir.ActivationFunctionType
AX = mybir.AxisListType

P = 128
TILES = 4
BLOCK = TILES * P
EPS = 1e-5
RSQRT_MAGIC = float(0x5F3759DF)
NEWTON = 3
LN_OPS = 7 + 3 * NEWTON
LN_SCALE = 2048.0
H_SCALE = 0.5
QUANT = 127.0


def gated_cross_attention_and_ffn(nc, x, ctx, g_xattn, g_ffn, W, b, w_gate, w_up, w_down, out):
    B, S, D = x.shape
    M = ctx.shape[1]
    HID = w_gate.shape[0]
    DC = D // P
    HC = HID // P
    BLOCKS = B * S // BLOCK
    ROWS = B * M
    RC = ROWS // P
    LOOPS = (BLOCKS - 4) // 2
    assert DC == 2 and RC == 2 and TILES * M <= 512 and S == 2 * BLOCK and HC == 6 and D <= 512

    x_v = x.rearrange("b s d -> (b s) d").rearrange("(k p j) d -> k p (j d)", p=P, j=TILES)
    out_v = out.rearrange("b s d -> (b s) d").rearrange("(k p j) d -> k p (j d)", p=P, j=TILES)

    with ExitStack() as stack:
        def sb(name, shape, dt):
            return stack.enter_context(nc.sbuf_tensor(name, shape, dt))

        def psum(name):
            return stack.enter_context(nc.psum_tensor(name, [P, 512], F32))

        def sem(name):
            return stack.enter_context(nc.semaphore(name))

        xs = sb("xs", [P, BLOCKS * TILES * D], F32)
        ident = sb("ident", [P, P], F32)
        ident16 = sb("ident16", [P, P], F16)
        W_nat = sb("W_nat", [P, DC, D], F32)
        W_T = sb("W_T", [P, DC, D], F32)
        b_col = sb("b_col", [P, DC], F32)
        b_rep = sb("b_rep", [P, DC, P], F32)
        ctx_nat = sb("ctx_nat", [P, RC, D], F32)
        ctx_T = sb("ctx_T", [P, DC, ROWS], F32)
        ctx_m = sb("ctx_m", [2 * M, B * D], F32)
        ctx_hi = sb("ctx_hi", [2 * M, B * D], F32R)
        ctx_lo = sb("ctx_lo", [2 * M, B * D], F32R)
        eo_T = sb("eo_T", [P, DC, ROWS], F32)
        key_T = sb("key_T", [P, DC, ROWS], F32)
        b_dot = sb("b_dot", [P, ROWS], F32)
        g_raw = sb("g_raw", [P, 2], F32)
        g_tanh = sb("g_tanh", [P, 2], F32)
        out_coef = sb("out_coef", [P, 1], F32)
        wg_int = sb("wg_int", [P, HC, D], I32)
        wu_int = sb("wu_int", [P, HC, D], I32)
        wd_int = sb("wd_int", [P, DC, HID], I32)
        wg16 = sb("wg16", [P, HC, D], F16)
        wu16 = sb("wu16", [P, HC, D], F16)
        wd16 = sb("wd16", [P, DC, HID], F16)
        wg_T = sb("wg_T", [P, DC, HID], F16)
        wu_T = sb("wu_T", [P, DC, HID], F16)
        wd_T = sb("wd_T", [P, HC, D], F16)

        stats = sb("stats", [P, 2, TILES, 6], F32)
        mean_sum = sb("mean_sum", [P, 2, TILES], F32)
        mean_gap = sb("mean_gap", [P, 2, TILES], F32)
        sq_sum = sb("sq_sum", [P, 2, TILES], F32)
        mean = sb("mean", [P, 2, TILES], F32)
        gap_sq = sb("gap_sq", [P, 2, TILES], F32)
        var_eps = sb("var_eps", [P, 2, TILES], F32)
        rsqrt = sb("rsqrt", [P, NEWTON + 1, 2, TILES], F32)
        rsqrt_sq = sb("rsqrt_sq", [P, NEWTON, 2, TILES], F32)
        rsqrt_res = sb("rsqrt_res", [P, NEWTON, 2, TILES], F32)
        xn1 = sb("xn1", [P, TILES, D], F32)
        xn2 = sb("xn2", [P, TILES, D], F32)
        xn1_T = sb("xn1_T", [P, DC, BLOCK], F32)
        scores = sb("scores", [P, TILES, M], F32)
        neg_max = sb("neg_max", [P, TILES], F32)
        probs = sb("probs", [P, TILES, M], F32)
        probs_hl = sb("probs_hl", [P, TILES, 2, M], F32R)
        prob_sum = sb("prob_sum", [P, TILES], F32)
        prob_rcp = sb("prob_rcp", [P, TILES], F32)
        attn_coef = sb("attn_coef", [P, TILES], F32)
        probs_T = sb("probs_T", [2 * M, BLOCK], F32R)
        xhi = sb("xhi", [P, DC, BLOCK], F16)
        xlo = sb("xlo", [P, DC, BLOCK], F16)
        silu = sb("silu", [P, 2, BLOCK], F32)
        h32 = sb("h32", [P, HC, BLOCK], F32)
        hhi = sb("hhi", [P, HC, BLOCK], F16)
        hlo = sb("hlo", [P, HC, BLOCK], F16)
        w_abs = sb("w_abs", [P, 3], F32)
        w_max = sb("w_max", [P, 1], F32)
        w_wide = sb("w_wide", [P, 1], F32)
        ones_col = sb("ones_col", [P, 1], F32)
        wide_flag = sb("wide_flag", [1, 1], I32)
        wgF_T = sb("wgF_T", [P, DC, HID], F32)
        wuF_T = sb("wuF_T", [P, DC, HID], F32)
        wdF_T = sb("wdF_T", [P, HC, D], F32)
        y_sb = sb("y_sb", [P, 2, TILES * D], F32)

        gate_ps = [psum("gate_ps0"), psum("gate_ps1")]
        up_ps = [psum("up_ps0"), psum("up_ps1")]
        out_ps = [psum("out_ps0"), psum("out_ps1")]
        att_ps = [psum("att_ps0"), psum("att_ps1")]

        x_in = [sem("x_in0"), sem("x_in1")]
        W_in, ctx_in, ctxm_in, b_in, g_in = sem("W_in"), sem("ctx_in"), sem("ctxm_in"), sem("b_in"), sem("g_in")
        wg_in, wu_in, wd_in = sem("wg_in"), sem("wu_in"), sem("wd_in")
        y_free = [sem("y_free0"), sem("y_free1")]
        ident_set, b_rep_set = sem("ident_set"), sem("b_rep_set")
        setup_T, setup_T_copied = sem("setup_T"), sem("setup_T_copied")
        eo_done, eo_copied = sem("eo_done"), sem("eo_copied")
        key_done, key_copied = sem("key_done"), sem("key_copied")
        bdot_done, bdot_copied = sem("bdot_done"), sem("bdot_copied")
        ones_set = sem("ones_set")
        tanh_done, coef_done = sem("tanh_done"), sem("coef_done")
        w16_ready = sem("w16_ready")
        wT_done = sem("wT_done")
        gate_free = sem("gate_free")
        up_free = sem("up_free")
        out_free = sem("out_free")
        bn_done, ln_math = sem("bn_done"), sem("ln_math")
        xn1_ready, xn2_ready = sem("xn1_ready"), sem("xn2_ready")
        t1_done, t1_copied = sem("t1_done"), sem("t1_copied")
        s_done, s_added, max_ready = sem("s_done"), sem("s_added"), sem("max_ready")
        probs_ready = sem("probs_ready")
        phi_ready, plo_ready = sem("phi_ready"), sem("plo_ready")
        ctx_split = sem("ctx_split")
        rcp_done, acoef_ready = sem("rcp_done"), sem("acoef_ready")
        pt_done, pt_copied = sem("pt_done"), sem("pt_copied")
        pv_done, x1_ready = sem("pv_done"), sem("x1_ready")
        t2_done, xhi_ready, xlo_ready = sem("t2_done"), sem("xhi_ready"), sem("xlo_ready")
        gu_done = sem("gu_done")
        hhi_ready, hlo_ready = sem("hhi_ready"), sem("hlo_ready")
        down_done = sem("down_done")
        abs_done, wide_col, wide_sum, flag_set = sem("abs_done"), sem("wide_col"), sem("wide_sum"), sem("flag_set")
        wf_ready, wfT_done, wfT_copied = sem("wf_ready"), sem("wfT_done"), sem("wfT_copied")
        gen_bn, gen_xn, gen_xT, gen_xT_copied = sem("gen_bn"), sem("gen_xn"), sem("gen_xT"), sem("gen_xT_copied")
        gen_gu, gen_silu, gen_h, gen_down, gen_y = sem("gen_gu"), sem("gen_silu"), sem("gen_h"), sem("gen_down"), sem("gen_y")

        def x_tile(k, j):
            return xs[:, bass.ds(k * (TILES * D) + j * D, D)]

        gate_up_banks = [gate_ps[0], gate_ps[1], up_ps[0]]
        h32_rows = h32[:].rearrange("p c n -> p (c n)")[:, 0:HC * D]

        CTX_PARTS = [(0, M), (M, ROWS - M)]
        key_banks = [(gate_ps[0], gate_ps[1], up_ps[0]), (out_ps[0], out_ps[1], up_ps[1])]

        def general_groups():
            flat = "p a b -> p (a b)"
            return ((wg_int[:].rearrange(flat), wgF_T[:].rearrange(flat), [(c * D + d * P) for d in range(DC) for c in range(HC)]),
                    (wu_int[:].rearrange(flat), wuF_T[:].rearrange(flat), [(c * D + d * P) for d in range(DC) for c in range(HC)]),
                    (wd_int[:].rearrange(flat), wdF_T[:].rearrange(flat), [(d * HID + c * P) for c in range(HC) for d in range(DC)]))

        FAST_STORES = 16 * (BLOCKS // 2 + 1)
        FAST_Y = 4 * BLOCKS + 2

        def weights_are_wide(eng):
            eng.wait_ge(flag_set, 1)
            return eng.value_load(wide_flag[0:1, 0:1], min_val=0, max_val=P) > 0

        block = stack.enter_context(nc.Block())

        @block.sync
        def _(sp):
            def load_x(k, par):
                sp.dma_start(xs[:, bass.ds(k * (TILES * D), TILES * D)], x_v[bass.ds(k, 1)].rearrange("k p f -> (k p) f")).then_inc(x_in[par], 16)

            def store_y(k, par):
                sp.wait_ge(out_free, 4 * k + 6)
                sp.dma_start(out_v[bass.ds(k, 1)].rearrange("k p f -> (k p) f"), y_sb[:, par]).then_inc(y_free[par], 16)

            load_x(0, 0)
            sp.dma_start(W_nat[:], W.rearrange("(c p) d -> p c d", p=P)).then_inc(W_in, 16)
            sp.dma_start(ctx_nat[:], ctx.rearrange("b m d -> (b m) d").rearrange("(c p) d -> p c d", p=P)).then_inc(ctx_in, 16)
            for half in range(2):
                sp.dma_start(ctx_m[half * M:(half + 1) * M].rearrange("m (b d) -> m b d", b=B),
                             ctx.rearrange("b m d -> m b d")).then_inc(ctxm_in, 16)
            load_x(1, 1)
            for par in range(2):
                sp.wait_ge(x_in[par], 16)
                load_x(2 + par, par)

            def step(k, i, par, load):
                if load:
                    sp.wait_ge(x_in[par], 16 * i + 32)
                    load_x(k + 4, par)
                store_y(k, par)

            with sp.Fori(0, LOOPS) as i:
                for par in range(2):
                    step(2 * i + par, i, par, True)
            for k in range(2 * LOOPS, BLOCKS):
                step(k, k // 2, k % 2, False)
            for par in range(2):
                sp.wait_ge(y_free[par], FAST_STORES)
            with sp.If(weights_are_wide(sp)):
                with sp.Fori(0, BLOCKS) as k:
                    sp.wait_ge(gen_y, 4 * k + 4)
                    sp.dma_start(out_v[bass.ds(k, 1)].rearrange("k p f -> (k p) f"), y_sb[:, 0]).then_inc(y_free[0], 16)
                sp.wait_ge(y_free[0], FAST_STORES + 16 * BLOCKS)

        @block.scalar
        def _(act):
            act.dma_start(b_col[:], b.rearrange("(c p) -> p c", p=P), allow_slow_non_contiguous=True).then_inc(b_in, 16)
            act.dma_start(wg_int[:], w_gate.rearrange("(c p) d -> p c d", p=P)).then_inc(wg_in, 16)
            act.dma_start(wu_int[:], w_up.rearrange("(c p) d -> p c d", p=P)).then_inc(wu_in, 16)
            act.dma_start(wd_int[:], w_down.rearrange("(c p) h -> p c h", p=P)).then_inc(wd_in, 16)
            act.dma_start(g_raw[:, 0:1], g_xattn.partition_broadcast(P)).then_inc(g_in, 16)
            act.dma_start(g_raw[:, 1:2], g_ffn.partition_broadcast(P)).then_inc(g_in, 16)

            def copy_t1(a):
                for c in range(DC):
                    act.wait_ge(t1_done, 2 * a + c + 1)
                    nc.scalar.copy(xn1_T[:, c], att_ps[c][:]).then_inc(t1_copied, 1)

            def exp_scores(a):
                act.wait_ge(max_ready, a + 1)
                for j in range(TILES):
                    last = nc.scalar.activation(probs[:, j], scores[:, j], ACT.Exp, bias=neg_max[:, j:j + 1],
                                                accum_out=prob_sum[:, j:j + 1])
                last.then_inc(probs_ready, 1)

            def copy_pt(a):
                act.wait_ge(pt_done, a + 1)
                nc.scalar.copy(probs_T[:], att_ps[1][:]).then_inc(pt_copied, 1)

            def x_high(a):
                for c in range(DC):
                    act.wait_ge(t2_done, 2 * a + c + 1)
                    nc.scalar.mul(xhi[:, c], att_ps[c][:], LN_SCALE).then_inc(xhi_ready, 1)

            def silu_gate(k, c):
                act.wait_ge(gu_done, 6 * k + c + 1)
                nc.scalar.activation(silu[:, c % 2], gate_ps[c % 2][:], ACT.Silu,
                                     scale=1.0 / (LN_SCALE * QUANT)).then_inc(gate_free, 1)

            def h_high(k, c):
                act.wait_ge(up_free, 6 * k + c + 3)
                nc.scalar.copy(hhi[:, c], h32[:, c]).then_inc(hhi_ready, 1)

            def copy_eo(part):
                act.wait_ge(eo_done, part + 1)
                lo, n = CTX_PARTS[part]
                for e in range(DC):
                    last = nc.scalar.activation(eo_T[:, e, lo:lo + n], key_banks[part][0][:, e * n:(e + 1) * n], ACT.Identity,
                                                bias=b_col[:, e:e + 1])
                last.then_inc(eo_copied, 1)

            def copy_key(part):
                act.wait_ge(key_done, part + 1)
                lo, n = CTX_PARTS[part]
                nc.scalar.copy(key_T[:, :, lo:lo + n], key_banks[part][1][:, 0:DC * n].rearrange("p (c n) -> p c n", c=DC)).then_inc(key_copied, 1)

            def copy_bdot(part):
                act.wait_ge(bdot_done, part + 1)
                lo, n = CTX_PARTS[part]
                nc.scalar.copy(b_dot[:, lo:lo + n], key_banks[part][2][:, 0:n]).then_inc(bdot_copied, 1)

            def to_f16(w_in, w16, w_int):
                act.wait_ge(w_in, 16)
                nc.scalar.copy(w16[:], w_int[:]).then_inc(w16_ready, 1)

            def copy_wT(dst, banks, done, first):
                for g in range(2):
                    act.wait_ge(wT_done, first + g + 1)
                    nc.scalar.copy(dst(g).bitcast(F32), banks[g][:, 0:HID // 2]).then_inc(done, 1)

            for n, (dst, bank) in enumerate(((W_T, att_ps[0]), (ctx_T, att_ps[1]))):
                act.wait_ge(setup_T, n + 1)
                nc.scalar.copy(dst[:].rearrange("p c e -> p (c e)"), bank[:]).then_inc(setup_T_copied, 1)
            act.wait_ge(b_in, 16)
            copy_eo(0)
            copy_key(0)
            copy_bdot(0)
            copy_t1(0)
            to_f16(wg_in, wg16, wg_int)
            copy_eo(1)
            act.wait_ge(g_in, 32)
            nc.scalar.activation(g_tanh[:], g_raw[:], ACT.Tanh).then_inc(tanh_done, 1)
            exp_scores(0)
            to_f16(wu_in, wu16, wu_int)
            copy_pt(0)
            copy_wT(lambda g: wg_T[:, g], gate_ps, gate_free, 0)
            to_f16(wd_in, wd16, wd_int)
            copy_key(1)
            copy_bdot(1)
            copy_wT(lambda g: wu_T[:, g], up_ps, up_free, 2)
            copy_t1(1)
            copy_wT(lambda g: wd_T[:, g * (HC // 2):(g + 1) * (HC // 2)].rearrange("p c d -> p (c d)"), out_ps, out_free, 4)
            x_high(0)
            exp_scores(1)

            def step(k, next1, next2):
                silu_gate(k, 0)
                silu_gate(k, 1)
                h_high(k, 0)
                if next1:
                    copy_pt(k + 1)
                silu_gate(k, 2)
                h_high(k, 1)
                silu_gate(k, 3)
                h_high(k, 2)
                silu_gate(k, 4)
                h_high(k, 3)
                if next2:
                    copy_t1(k + 2)
                silu_gate(k, 5)
                h_high(k, 4)
                h_high(k, 5)
                if next1:
                    x_high(k + 1)
                if next2:
                    exp_scores(k + 2)

            with act.Fori(0, LOOPS) as i:
                for par in range(2):
                    step(2 * i + par, True, True)
            for k in range(2 * LOOPS, BLOCKS):
                step(k, k + 1 < BLOCKS, k + 2 < BLOCKS)

            with act.If(weights_are_wide(act)):
                act.wait_ge(out_free, FAST_Y)
                with act.Fori(0, BLOCKS) as k:
                    for j in range(TILES):
                        act.wait_ge(gen_gu, 4 * k + j + 1)
                        for g, (bank, n) in enumerate(zip(gate_ps, (512, HID - 512))):
                            last = nc.scalar.activation(silu[:].rearrange("p a n -> p (a n)")[:, g * 512:g * 512 + n],
                                                        bank[:, 0:n], ACT.Silu)
                        last.then_inc(gen_silu, 1)

        @block.gpsimd
        def _(pool):
            nc.gpsimd.memset(ident[:], 0.0).then_inc(ident_set, 1)
            pool.wait_ge(ident_set, 1)
            nc.gpsimd.affine_select(out=ident[:], in_=ident[:], compare_op=ALU.not_equal, fill=1.0, base=0,
                                    pattern=[[-1, P]], channel_multiplier=1).then_inc(ident_set, 1)
            pool.wait_ge(ident_set, 2)
            nc.gpsimd.tensor_copy(ident16[:], ident[:]).then_inc(ident_set, 1)

            def h_low(k, c):
                pool.wait_ge(hhi_ready, 6 * k + c + 1)
                nc.gpsimd.tensor_tensor(hlo[:, c], h32[:, c], hhi[:, c], ALU.subtract).then_inc(hlo_ready, 1)

            pool.wait_ge(b_in, 16)
            for c in range(DC):
                nc.gpsimd.tensor_copy(b_rep[:, c], b_col[:, c:c + 1].broadcast_to([P, P])).then_inc(b_rep_set, 1)
            pool.wait_ge(ctxm_in, 32)
            nc.gpsimd.tensor_copy(ctx_hi[:], ctx_m[:]).then_inc(ctx_split, 1)
            pool.wait_ge(ctx_split, 1)
            nc.gpsimd.tensor_tensor(ctx_lo[:], ctx_m[:], ctx_hi[:].bitcast(F32), ALU.subtract).then_inc(ctx_split, 1)

            with pool.Fori(0, BLOCKS) as k:
                for c in range(HC):
                    h_low(k, c)

        @block.vector
        def _(dve):
            def norm_stats(k, w):
                for j in range(TILES):
                    last = nc.vector.bn_stats(stats[:, w, j], x_tile(k, j))
                last.then_inc(bn_done, 1)

            def norm_factors(m, half, stats_needed, stats_sem=bn_done):
                n = LN_OPS * m
                even, odd = stats[:, half, :, 0:3], stats[:, half, :, 3:6]
                v = nc.vector
                dve.wait_ge(stats_sem, stats_needed)
                v.tensor_tensor(mean_sum[:, half], even[:, :, :, 1], odd[:, :, :, 1], ALU.add).then_inc(ln_math, 1)
                v.tensor_tensor(mean_gap[:, half], even[:, :, :, 1], odd[:, :, :, 1], ALU.subtract).then_inc(ln_math, 1)
                v.scalar_tensor_tensor(out=sq_sum[:, half], in0=even[:, :, :, 2], scalar=EPS * D, in1=odd[:, :, :, 2],
                                       op0=ALU.add, op1=ALU.add).then_inc(ln_math, 1)
                dve.wait_ge(ln_math, n + 2)
                v.scalar_tensor_tensor(out=gap_sq[:, half], in0=mean_gap[:, half], scalar=0.25, in1=mean_gap[:, half],
                                       op0=ALU.mult, op1=ALU.mult).then_inc(ln_math, 1)
                v.tensor_scalar(mean[:, half], mean_sum[:, half], 0.5, None, ALU.mult).then_inc(ln_math, 1)
                dve.wait_ge(ln_math, n + 4)
                v.scalar_tensor_tensor(out=var_eps[:, half], in0=sq_sum[:, half], scalar=1.0 / D, in1=gap_sq[:, half],
                                       op0=ALU.mult, op1=ALU.add).then_inc(ln_math, 1)
                dve.wait_ge(ln_math, n + 6)
                v.tensor_scalar(rsqrt[:, 0, half].bitcast(I32), var_eps[:, half].bitcast(I32), -0.5, RSQRT_MAGIC,
                                ALU.mult, ALU.add).then_inc(ln_math, 1)
                for t in range(NEWTON):
                    y = rsqrt[:, t, half]
                    dve.wait_ge(ln_math, n + 7 + 3 * t)
                    v.tensor_tensor(rsqrt_sq[:, t, half], y, y, ALU.mult).then_inc(ln_math, 1)
                    dve.wait_ge(ln_math, n + 8 + 3 * t)
                    v.scalar_tensor_tensor(out=rsqrt_res[:, t, half], in0=rsqrt_sq[:, t, half], scalar=-0.5,
                                           in1=var_eps[:, half], op0=ALU.mult, op1=ALU.mult).then_inc(ln_math, 1)
                    dve.wait_ge(ln_math, n + 9 + 3 * t)
                    v.scalar_tensor_tensor(out=rsqrt[:, t + 1, half], in0=rsqrt_res[:, t, half], scalar=1.5, in1=y,
                                           op0=ALU.add, op1=ALU.mult).then_inc(ln_math, 1)

            def normalise(k, dst, m, w, ready):
                dve.wait_ge(ln_math, LN_OPS * (m + 1))
                for j in range(TILES):
                    last = nc.vector.tensor_scalar(dst[:, j], x_tile(k, j), mean[:, w, j:j + 1],
                                                   rsqrt[:, NEWTON, w, j:j + 1], ALU.subtract, ALU.mult)
                last.then_inc(ready, 1)

            def row_max(a, batch):
                dve.wait_ge(s_done, a + 1)
                bd = b_dot[:, bass.ds(batch * M, M)].unsqueeze(1).broadcast_to([P, TILES, M])
                nc.vector.tensor_tensor(scores[:], att_ps[0][:, 0:TILES * M].rearrange("p (j m) -> p j m", j=TILES),
                                        bd, ALU.add).then_inc(s_added, 1)
                dve.wait_ge(s_added, a + 1)
                nc.vector.tensor_reduce(neg_max[:], scores[:], AX.X, ALU.max, negate=True).then_inc(max_ready, 1)

            def split_probs(a):
                dve.wait_ge(probs_ready, a + 1)
                nc.vector.tensor_copy(probs_hl[:, :, 0], probs[:]).then_inc(phi_ready, 1)
                dve.wait_ge(phi_ready, a + 1)
                nc.vector.tensor_tensor(probs_hl[:, :, 1], probs[:], probs_hl[:, :, 0].bitcast(F32),
                                        ALU.subtract).then_inc(plo_ready, 1)
                nc.vector.reciprocal(prob_rcp[:], prob_sum[:]).then_inc(rcp_done, 1)
                dve.wait_ge(rcp_done, a + 1)
                nc.vector.tensor_scalar(attn_coef[:], prob_rcp[:], g_tanh[:, 0:1], None, ALU.mult).then_inc(acoef_ready, 1)

            def add_attention(a):
                dve.wait_ge(acoef_ready, a + 1)
                for j in range(TILES):
                    if j % 2 == 0:
                        dve.wait_ge(pv_done, 2 * a + j // 2 + 1)
                    last = nc.vector.scalar_tensor_tensor(out=x_tile(a, j), in0=att_ps[j // 2][:, (j % 2) * D:(j % 2 + 1) * D],
                                                          scalar=attn_coef[:, j:j + 1], in1=x_tile(a, j),
                                                          op0=ALU.mult, op1=ALU.add)
                last.then_inc(x1_ready, 1)

            def x_low(a):
                for c in range(DC):
                    dve.wait_ge(xhi_ready, 2 * a + c + 1)
                    nc.vector.scalar_tensor_tensor(out=xlo[:, c], in0=att_ps[c][:], scalar=LN_SCALE, in1=xhi[:, c],
                                                   op0=ALU.mult, op1=ALU.subtract).then_inc(xlo_ready, 1)

            def h_of(k, c):
                dve.wait_ge(gate_free, 6 * k + c + 3)
                nc.vector.scalar_tensor_tensor(out=h32[:, c], in0=up_ps[c % 2][:], scalar=H_SCALE / (LN_SCALE * QUANT),
                                               in1=silu[:, c % 2], op0=ALU.mult, op1=ALU.mult).then_inc(up_free, 1)

            def add_ffn(k, i, par):
                dve.wait_ge(y_free[par], 16 * i + 16)
                for j in range(TILES):
                    if j % 2 == 0:
                        dve.wait_ge(down_done, 2 * k + j // 2 + 1)
                    nc.vector.scalar_tensor_tensor(out=y_sb[:, par, j * D:(j + 1) * D],
                                                   in0=out_ps[j // 2][:, (j % 2) * D:(j % 2 + 1) * D],
                                                   scalar=out_coef[:, 0:1], in1=x_tile(k, j),
                                                   op0=ALU.mult, op1=ALU.add).then_inc(out_free, 1)

            nc.vector.memset(ones_col[:], 1.0).then_inc(ones_set, 1)
            for half in range(2):
                nc.vector.memset(y_sb[:, half, 0:1], 0.0).then_inc(y_free[half], 16)
            dve.wait_ge(x_in[0], 16)
            norm_stats(0, 0)
            norm_factors(0, slice(0, 1), 1)
            normalise(0, xn1, 0, 0, xn1_ready)
            dve.wait_ge(x_in[1], 16)
            norm_stats(1, 0)
            norm_factors(1, slice(0, 1), 2)
            dve.wait_ge(bdot_copied, 1)
            row_max(0, 0)
            dve.wait_ge(t1_done, 2)
            normalise(1, xn1, 1, 0, xn1_ready)
            dve.wait_ge(tanh_done, 1)
            nc.vector.tensor_scalar(out_coef[:], g_tanh[:, 1:2], 1.0 / (H_SCALE * QUANT), None, ALU.mult).then_inc(coef_done, 1)
            split_probs(0)
            dve.wait_ge(x_in[0], 32)
            norm_stats(2, 0)
            add_attention(0)
            dve.wait_ge(x1_ready, 1)
            norm_stats(0, 1)
            norm_factors(2, slice(0, 2), 4)
            normalise(0, xn2, 2, 1, xn2_ready)
            row_max(1, 0)
            x_low(0)
            normalise(2, xn1, 2, 0, xn1_ready)
            dve.wait_ge(coef_done, 1)
            dve.wait_ge(bdot_copied, 2)

            def largest_weight(n):
                w_int = (wg_int, wu_int, wd_int)[n]
                nc.vector.tensor_reduce(w_abs[:, n:n + 1], w_int[:], AX.XY, ALU.max, apply_absolute_value=True).then_inc(abs_done, 1)

            def find_wide_weights():
                dve.wait_ge(abs_done, 3)
                nc.vector.tensor_reduce(w_max[:], w_abs[:], AX.X, ALU.max).then_inc(abs_done, 1)
                dve.wait_ge(abs_done, 4)
                nc.vector.tensor_scalar(w_wide[:], w_max[:], QUANT, None, ALU.is_gt).then_inc(wide_col, 1)

            def step(k, i, par, batch2, next1, next2, next3, bn_count):
                if next1:
                    split_probs(k + 1)
                h_of(k, 0)
                if not next1:
                    largest_weight(0)
                if next3:
                    dve.wait_ge(x_in[1 - par], 16 * (i + par) + 32)
                h_of(k, 1)
                if next3:
                    norm_stats(k + 3, 0)
                if not next1:
                    largest_weight(1)
                h_of(k, 2)
                if next1:
                    add_attention(k + 1)
                    dve.wait_ge(x1_ready, k + 2)
                else:
                    largest_weight(2)
                h_of(k, 3)
                if next1:
                    norm_stats(k + 1, 1)
                    norm_factors(k + 3, slice(0 if next3 else 1, 2), bn_count)
                else:
                    find_wide_weights()
                h_of(k, 4)
                if next1:
                    normalise(k + 1, xn2, k + 3, 1, xn2_ready)
                h_of(k, 5)
                if next2:
                    row_max(k + 2, batch2)
                if next1:
                    x_low(k + 1)
                else:
                    dve.wait_ge(wide_sum, 1)
                    nc.vector.tensor_copy(wide_flag[:], att_ps[0][0:1, 0:1]).then_inc(flag_set, 1)
                if next3:
                    normalise(k + 3, xn1, k + 3, 0, xn1_ready)
                add_ffn(k, i, par)

            with dve.Fori(0, LOOPS) as i:
                for par in range(2):
                    step(2 * i + par, i, par, i + 1, True, True, True, 4 * i + 2 * par + 6)
            for k in range(2 * LOOPS, BLOCKS):
                bn_count = sum(a + 3 < BLOCKS for a in range(k + 1)) + sum(a + 1 < BLOCKS for a in range(k + 1)) + 4
                step(k, k // 2, k % 2, k // 2 + 1, k + 1 < BLOCKS, k + 2 < BLOCKS, k + 3 < BLOCKS, bn_count)

            with dve.If(weights_are_wide(dve)):
                dve.wait_ge(out_free, FAST_Y)
                groups = general_groups()
                for n, (w_int, _, _) in enumerate(groups):
                    if n:
                        dve.wait_ge(wfT_done, 3 * n)
                    nc.vector.tensor_scalar(h32_rows, w_int, 1.0 / QUANT, None, ALU.mult).then_inc(wf_ready, 1)
                    for g in range(3):
                        dve.wait_ge(wfT_done, 3 * n + g + 1)
                        nc.vector.tensor_copy(groups[n][1][:, g * 512:(g + 1) * 512], gate_up_banks[g][:]).then_inc(wfT_copied, 1)

                def general_tile(k, j):
                    t = 4 * k + j
                    nc.vector.bn_stats(stats[:, 0, 0], x_tile(k, j)).then_inc(gen_bn, 1)
                    norm_factors(BLOCKS + 2 + t, slice(0, 1), t + 1, gen_bn)
                    dve.wait_ge(ln_math, LN_OPS * (BLOCKS + 3 + t))
                    nc.vector.tensor_scalar(xn1[:, 0], x_tile(k, j), mean[:, 0, 0:1], rsqrt[:, NEWTON, 0, 0:1],
                                            ALU.subtract, ALU.mult).then_inc(gen_xn, 1)
                    dve.wait_ge(gen_xT, t + 1)
                    nc.vector.tensor_copy(xn1_T[:, 0, 0:D], att_ps[0][:, 0:D]).then_inc(gen_xT_copied, 1)
                    dve.wait_ge(gen_silu, t + 1)
                    for g, (bank, n) in enumerate(zip(up_ps, (512, HID - 512))):
                        last = nc.vector.tensor_tensor(h32[:].rearrange("p c n -> p (c n)")[:, g * 512:g * 512 + n], bank[:, 0:n],
                                                       silu[:].rearrange("p a n -> p (a n)")[:, g * 512:g * 512 + n], ALU.mult)
                    last.then_inc(gen_h, 1)
                    if j == 0:
                        dve.wait_ge(y_free[0], 16 * k + FAST_STORES)
                    dve.wait_ge(gen_down, t + 1)
                    nc.vector.scalar_tensor_tensor(out=y_sb[:, 0, j * D:(j + 1) * D], in0=out_ps[0][:, 0:D],
                                                   scalar=g_tanh[:, 1:2], in1=x_tile(k, j), op0=ALU.mult, op1=ALU.add).then_inc(gen_y, 1)

                with dve.Fori(0, BLOCKS) as k:
                    for j in range(TILES):
                        general_tile(k, j)

        @block.tensor
        def _(pe):
            mm = nc.tensor.matmul

            def t1(a, after_attention=True):
                if after_attention:
                    pe.wait_ge(x1_ready, a)
                pe.wait_ge(xn1_ready, a + 1)
                for c in range(DC):
                    for j in range(TILES):
                        last = nc.tensor.transpose(att_ps[c][:, j * P:(j + 1) * P], xn1[:, j, c * P:(c + 1) * P], ident[:])
                    last.then_inc(t1_done, 1)

            def score(a, batch):
                pe.wait_ge(t1_copied, 2 * a + 2)
                for j in range(TILES):
                    for c in range(DC):
                        last = mm(att_ps[0][:, j * M:(j + 1) * M], xn1_T[:, c, j * P:(j + 1) * P],
                                  key_T[:, c, bass.ds(batch * M, M)], start=(c == 0), stop=(c == DC - 1))
                last.then_inc(s_done, 1)

            def transpose_probs(a):
                pe.wait_ge(plo_ready, a + 1)
                for j in range(TILES):
                    last = nc.tensor.transpose(att_ps[1][:, j * P:(j + 1) * P],
                                               probs_hl[:, j].rearrange("p h m -> p (h m)").bitcast(F32), ident[:])
                last.then_inc(pt_done, 1)

            def attend(a, batch):
                pe.wait_ge(pt_copied, a + 1)
                for j in range(TILES):
                    for n, c_half in enumerate((ctx_hi, ctx_lo)):
                        last = mm(att_ps[j // 2][:, (j % 2) * D:(j % 2 + 1) * D], probs_T[:, j * P:(j + 1) * P],
                                  c_half[:, bass.ds(batch * D, D)], start=(n == 0), stop=(n == 1))
                    if j % 2 == 1:
                        last.then_inc(pv_done, 1)

            def t2(a, after_score=True):
                if after_score:
                    pe.wait_ge(s_added, a + 2)
                pe.wait_ge(xn2_ready, a + 1)
                for c in range(DC):
                    for j in range(TILES):
                        last = nc.tensor.transpose(att_ps[c][:, j * P:(j + 1) * P], xn2[:, j, c * P:(c + 1) * P], ident[:])
                    last.then_inc(t2_done, 1)

            def gate_up(k, c):
                if c == 0:
                    pe.wait_ge(xhi_ready, 2 * k + 2)
                pe.wait_ge(gate_free, 6 * k + c + 1)
                pe.wait_ge(up_free, 6 * k + c + 1)
                for w_T, bank in ((wg_T, gate_ps[c % 2]), (wu_T, up_ps[c % 2])):
                    for n, half in enumerate((xhi, xlo)):
                        if c == 0 and n == 1 and w_T is wg_T:
                            pe.wait_ge(xlo_ready, 2 * k + 2)
                        for d in range(DC):
                            last = mm(bank[:], w_T[:, d, c * P:(c + 1) * P], half[:, d],
                                      start=(n == 0 and d == 0), stop=(n == 1 and d == DC - 1))
                last.then_inc(gu_done, 1)

            def down(k, c):
                if c == 0:
                    pe.wait_ge(out_free, 4 * k + 2)
                pe.wait_ge(hlo_ready, 6 * k + c + 1)
                for j in range(TILES):
                    for n, half in enumerate((hhi, hlo)):
                        last = mm(out_ps[j // 2][:, (j % 2) * D:(j % 2 + 1) * D], half[:, c, j * P:(j + 1) * P], wd_T[:, c],
                                  start=(c == 0 and n == 0 and j % 2 == 0), stop=(c == HC - 1 and n == 1),
                                  skip_group_check=True)
                    if c == HC - 1 and j % 2 == 1:
                        last.then_inc(down_done, 1)

            def context_out(part):
                lo, n = CTX_PARTS[part]
                for e in range(DC):
                    for d in range(DC):
                        last = mm(key_banks[part][0][:, e * n:(e + 1) * n], W_T[:, d, e * P:(e + 1) * P], ctx_T[:, d, lo:lo + n],
                                  start=(d == 0), stop=(d == DC - 1))
                last.then_inc(eo_done, 1)

            def keys(part):
                pe.wait_ge(eo_copied, part + 1)
                lo, n = CTX_PARTS[part]
                for d in range(DC):
                    for e in range(DC):
                        last = mm(key_banks[part][1][:, d * n:(d + 1) * n], W_nat[:, e, d * P:(d + 1) * P], eo_T[:, e, lo:lo + n],
                                  start=(e == 0), stop=(e == DC - 1))
                last.then_inc(key_done, 1)

            def b_dots(part):
                lo, n = CTX_PARTS[part]
                for e in range(DC):
                    last = mm(key_banks[part][2][:, 0:n], b_rep[:, e], eo_T[:, e, lo:lo + n], start=(e == 0), stop=(e == DC - 1))
                last.then_inc(bdot_done, 1)

            def transpose_gate_or_up(w16, banks, n):
                pe.wait_ge(w16_ready, n)
                for d in range(DC):
                    o = banks[d][:].bitcast(F16)
                    for c in range(HC):
                        last = nc.tensor.transpose(o[:, c * P:(c + 1) * P], w16[:, c, d * P:(d + 1) * P], ident16[:])
                    last.then_inc(wT_done, 1)

            def transpose_down():
                pe.wait_ge(w16_ready, 3)
                for g in range(2):
                    o = out_ps[g][:].bitcast(F16)
                    for c in range(HC // 2):
                        for d in range(DC):
                            h0 = (g * (HC // 2) + c) * P
                            last = nc.tensor.transpose(o[:, (c * DC + d) * P:(c * DC + d + 1) * P], wd16[:, d, h0:h0 + P], ident16[:])
                    last.then_inc(wT_done, 1)

            pe.wait_ge(ident_set, 3)
            for srcs, ready, bank in ((W_nat, W_in, 0), (ctx_nat, ctx_in, 1)):
                pe.wait_ge(ready, 16)
                for d in range(DC):
                    for r in range(2):
                        o = d * 2 * P + r * P
                        last = nc.tensor.transpose(att_ps[bank][:, o:o + P], srcs[:, r, d * P:(d + 1) * P], ident[:])
                last.then_inc(setup_T, 1)
            pe.wait_ge(setup_T_copied, 2)
            context_out(0)
            keys(0)
            pe.wait_ge(b_rep_set, 2)
            b_dots(0)
            t1(0, False)
            pe.wait_ge(key_copied, 1)
            score(0, 0)
            context_out(1)
            pe.wait_ge(bdot_copied, 1)
            transpose_gate_or_up(wg16, gate_ps, 1)
            keys(1)
            b_dots(1)
            transpose_probs(0)
            pe.wait_ge(ctx_split, 2)
            attend(0, 0)
            pe.wait_ge(bdot_copied, 2)
            transpose_gate_or_up(wu16, up_ps, 2)
            t1(1)
            transpose_down()
            score(1, 0)
            t2(0)

            def step(k, batch1, batch2, next1, next2):
                gate_up(k, 0)
                gate_up(k, 1)
                if next1:
                    transpose_probs(k + 1)
                gate_up(k, 2)
                if next1:
                    attend(k + 1, batch1)
                gate_up(k, 3)
                gate_up(k, 4)
                if next2:
                    t1(k + 2)
                gate_up(k, 5)
                if next2:
                    score(k + 2, batch2)
                for c in range(3):
                    down(k, c)
                if next1:
                    t2(k + 1, next2)
                else:
                    pe.wait_ge(wide_col, 1)
                    pe.wait_ge(ones_set, 1)
                    mm(att_ps[0][0:1, 0:1], w_wide[:], ones_col[:], start=True, stop=True).then_inc(wide_sum, 1)
                for c in range(3, HC):
                    down(k, c)

            with pe.Fori(0, LOOPS) as i:
                for par in range(2):
                    step(2 * i + par, i + par, i + 1, True, True)
            for k in range(2 * LOOPS, BLOCKS):
                step(k, (k + 1) // 2, k // 2 + 1, k + 1 < BLOCKS, k + 2 < BLOCKS)

            with pe.If(weights_are_wide(pe)):
                pe.wait_ge(out_free, FAST_Y)
                for n, (_, _, blocks) in enumerate(general_groups()):
                    pe.wait_ge(wf_ready, n + 1)
                    for g in range(3):
                        if n:
                            pe.wait_ge(wfT_copied, 3 * (n - 1) + g + 1)
                        for q in range(4):
                            at = blocks[4 * g + q]
                            last = nc.tensor.transpose(gate_up_banks[g][:, q * P:(q + 1) * P], h32_rows[:, at:at + P], ident[:])
                        last.then_inc(wfT_done, 1)
                pe.wait_ge(wfT_copied, 9)
                with pe.Fori(0, BLOCKS) as k:
                    for j in range(TILES):
                        t = 4 * k + j
                        pe.wait_ge(gen_xn, t + 1)
                        for d in range(DC):
                            last = nc.tensor.transpose(att_ps[0][:, d * P:(d + 1) * P], xn1[:, 0, d * P:(d + 1) * P], ident[:])
                        last.then_inc(gen_xT, 1)
                        pe.wait_ge(gen_xT_copied, t + 1)
                        for w_T, banks in ((wgF_T, gate_ps), (wuF_T, up_ps)):
                            for c in range(HC):
                                for d in range(DC):
                                    last = mm(banks[c // 4][:, c % 4 * P:(c % 4 + 1) * P], w_T[:, d, c * P:(c + 1) * P],
                                              xn1_T[:, 0, d * P:(d + 1) * P], start=(d == 0), stop=(d == DC - 1))
                        last.then_inc(gen_gu, 1)
                        pe.wait_ge(gen_h, t + 1)
                        for c in range(HC):
                            last = mm(out_ps[0][:, 0:D], h32[:].rearrange("p c n -> p (c n)")[:, c * P:(c + 1) * P], wdF_T[:, c],
                                      start=(c == 0), stop=(c == HC - 1))
                        last.then_inc(gen_down, 1)


_INS = ["x", "ctx_1024", "g_xattn", "g_ffn", "L0_xattn_W", "L0_xattn_b", "L0_ffn_w_gate", "L0_ffn_w_up", "L0_ffn_w_down"]


def kernel(**inputs):
    import numpy as np
    import concourse.bacc as bacc
    from concourse import mybir as mb
    from concourse.bass_utils import run_bass_kernel_spmd as run

    nc = bacc.Bacc("TRN2", target_bir_lowering=False, num_devices=1)
    arrays, args = {}, []
    for name in _INS:
        a = np.ascontiguousarray(inputs[name])
        arrays[f"in_{name}"] = a
        args.append(nc.dram_tensor(f"in_{name}", a.shape, mb.dt.from_np(a.dtype), kind="ExternalInput").ap())
    x = arrays["in_x"]
    o = nc.dram_tensor("out_y", x.shape, mb.dt.float32, kind="ExternalOutput").ap()
    gated_cross_attention_and_ffn(nc, *args, o)
    r = run(nc, [arrays], core_ids=[0])
    return r.results[0]["out_y"]
```

```python
from contextlib import ExitStack

import concourse.bass as bass
from concourse import mybir

F32 = mybir.dt.float32
F32R = mybir.dt.float32r
F16 = mybir.dt.float16
I32 = mybir.dt.int32
ALU = mybir.AluOpType
ACT = mybir.ActivationFunctionType
AX = mybir.AxisListType

P = 128
TILES = 4
BLOCK = TILES * P
EPS = 1e-5
RSQRT_MAGIC = float(0x5F3759DF)
NEWTON = 3
LN_OPS = 7 + 3 * NEWTON
LN_SCALE = 2048.0
H_SCALE = 0.5
QUANT = 127.0


def gated_cross_attention_and_ffn(nc, x, ctx, g_xattn, g_ffn, W, b, w_gate, w_up, w_down, out):
    B, S, D = x.shape
    M = ctx.shape[1]
    HID = w_gate.shape[0]
    DC = D // P
    HC = HID // P
    BLOCKS = B * S // BLOCK
    ROWS = B * M
    RC = ROWS // P
    LOOPS = (BLOCKS - 4) // 2
    assert DC == 2 and RC == 2 and TILES * M <= 512 and S == 2 * BLOCK and HC == 6 and D <= 512

    x_v = x.rearrange("b s d -> (b s) d").rearrange("(k p j) d -> k p (j d)", p=P, j=TILES)
    ctx_rows = ctx.rearrange("b m d -> (b m) d").rearrange("(c p) d -> p c d", p=P)
    out_v = out.rearrange("b s d -> (b s) d").rearrange("(k p j) d -> k p (j d)", p=P, j=TILES)

    with ExitStack() as stack:
        def sb(name, shape, dt):
            return stack.enter_context(nc.sbuf_tensor(name, shape, dt))

        def psum(name):
            return stack.enter_context(nc.psum_tensor(name, [P, 512], F32))

        def sem(name):
            return stack.enter_context(nc.semaphore(name))

        xs = sb("xs", [P, BLOCKS * TILES * D], F32)
        ident = sb("ident", [P, P], F32)
        ident16 = sb("ident16", [P, P], F16)
        W_nat = sb("W_nat", [P, DC, D], F32)
        W_T = sb("W_T", [P, DC, D], F32)
        b_col = sb("b_col", [P, DC], F32)
        b_rep = sb("b_rep", [P, DC, P], F32)
        ctx_nat = sb("ctx_nat", [P, RC, D], F32)
        ctx_T = sb("ctx_T", [P, DC, ROWS], F32)
        ctx_m = sb("ctx_m", [2 * M, B * D], F32)
        ctx_hi = sb("ctx_hi", [2 * M, B * D], F32R)
        ctx_lo = sb("ctx_lo", [2 * M, B * D], F32R)
        eo_T = sb("eo_T", [P, DC, ROWS], F32)
        key_T = sb("key_T", [P, DC, ROWS], F32)
        b_dot = sb("b_dot", [P, ROWS], F32)
        g_raw = sb("g_raw", [P, 2], F32)
        g_tanh = sb("g_tanh", [P, 2], F32)
        out_coef = sb("out_coef", [P, 1], F32)
        wg_int = sb("wg_int", [P, HC, D], I32)
        wu_int = sb("wu_int", [P, HC, D], I32)
        wd_int = sb("wd_int", [P, DC, HID], I32)
        wg16 = sb("wg16", [P, HC, D], F16)
        wu16 = sb("wu16", [P, HC, D], F16)
        wd16 = sb("wd16", [P, DC, HID], F16)
        wg_T = sb("wg_T", [P, DC, HID], F16)
        wu_T = sb("wu_T", [P, DC, HID], F16)
        wd_T = sb("wd_T", [P, HC, D], F16)

        stats = sb("stats", [P, 2, TILES, 6], F32)
        mean_sum = sb("mean_sum", [P, 2, TILES], F32)
        mean_gap = sb("mean_gap", [P, 2, TILES], F32)
        sq_sum = sb("sq_sum", [P, 2, TILES], F32)
        mean = sb("mean", [P, 2, TILES], F32)
        gap_sq = sb("gap_sq", [P, 2, TILES], F32)
        var_eps = sb("var_eps", [P, 2, TILES], F32)
        rsqrt = sb("rsqrt", [P, NEWTON + 1, 2, TILES], F32)
        rsqrt_sq = sb("rsqrt_sq", [P, NEWTON, 2, TILES], F32)
        rsqrt_res = sb("rsqrt_res", [P, NEWTON, 2, TILES], F32)
        xn1 = sb("xn1", [P, TILES, D], F32)
        xn2 = sb("xn2", [P, TILES, D], F32)
        xn1_T = sb("xn1_T", [P, DC, BLOCK], F32)
        scores = sb("scores", [P, TILES, M], F32)
        neg_max = sb("neg_max", [P, TILES], F32)
        probs = sb("probs", [P, TILES, M], F32)
        probs_hl = sb("probs_hl", [P, TILES, 2, M], F32R)
        prob_sum = sb("prob_sum", [P, TILES], F32)
        prob_rcp = sb("prob_rcp", [P, TILES], F32)
        attn_coef = sb("attn_coef", [P, TILES], F32)
        probs_T = sb("probs_T", [2 * M, BLOCK], F32R)
        xhi = sb("xhi", [P, DC, BLOCK], F16)
        xlo = sb("xlo", [P, DC, BLOCK], F16)
        silu = sb("silu", [P, 2, BLOCK], F32)
        h32 = sb("h32", [P, HC, BLOCK], F32)
        hhi = sb("hhi", [P, HC, BLOCK], F16)
        hlo = sb("hlo", [P, HC, BLOCK], F16)
        w_abs = sb("w_abs", [P, 3], F32)
        w_max = sb("w_max", [P, 1], F32)
        w_wide = sb("w_wide", [P, 1], F32)
        table_probe = sb("table_probe", [P, 1], F32)
        ones_col = sb("ones_col", [P, 1], F32)
        wide_flag = sb("wide_flag", [1, 1], I32)
        wgF_T = sb("wgF_T", [P, DC, HID], F32)
        wuF_T = sb("wuF_T", [P, DC, HID], F32)
        wdF_T = sb("wdF_T", [P, HC, D], F32)
        y_sb = sb("y_sb", [P, 2, TILES * D], F32)

        gate_ps = [psum("gate_ps0"), psum("gate_ps1")]
        up_ps = [psum("up_ps0"), psum("up_ps1")]
        out_ps = [psum("out_ps0"), psum("out_ps1")]
        att_ps = [psum("att_ps0"), psum("att_ps1")]

        x_in = [sem("x_in0"), sem("x_in1")]
        ctx_in = [sem("ctx_in0"), sem("ctx_in1")]
        W_in, ctxm_in, b_in, g_in = sem("W_in"), sem("ctxm_in"), sem("b_in"), sem("g_in")
        wg_in, wu_in, wd_in = sem("wg_in"), sem("wu_in"), sem("wd_in")
        y_free = [sem("y_free0"), sem("y_free1")]
        ident_set, b_rep_set = sem("ident_set"), sem("b_rep_set")
        setup_T, W_T_copied, ctx_T_copied = sem("setup_T"), sem("W_T_copied"), sem("ctx_T_copied")
        eo_done, eo_copied = sem("eo_done"), sem("eo_copied")
        key_done, key_copied = sem("key_done"), sem("key_copied")
        bdot_done, bdot_copied = sem("bdot_done"), sem("bdot_copied")
        ones_set = sem("ones_set")
        tanh_done, coef_done = sem("tanh_done"), sem("coef_done")
        wg16_ready, wu16_ready, wd16_ready = sem("wg16_ready"), sem("wu16_ready"), sem("wd16_ready")
        wT_done = sem("wT_done")
        gate_free = sem("gate_free")
        up_free = sem("up_free")
        out_free = sem("out_free")
        bn_done, ln_math = sem("bn_done"), sem("ln_math")
        xn1_ready, xn2_ready = sem("xn1_ready"), sem("xn2_ready")
        t1_done, t1_copied = sem("t1_done"), sem("t1_copied")
        s_done, s_added, max_ready = sem("s_done"), sem("s_added"), sem("max_ready")
        probs_ready = sem("probs_ready")
        phi_ready, plo_ready = sem("phi_ready"), sem("plo_ready")
        ctx_split = sem("ctx_split")
        rcp_done, acoef_ready = sem("rcp_done"), sem("acoef_ready")
        pt_done, pt_copied = sem("pt_done"), sem("pt_copied")
        pv_done, x1_ready = sem("pv_done"), sem("x1_ready")
        t2_done, xhi_ready, xlo_ready = sem("t2_done"), sem("xhi_ready"), sem("xlo_ready")
        gu_done = sem("gu_done")
        hhi_ready, hlo_ready = sem("hhi_ready"), sem("hlo_ready")
        down_done = sem("down_done")
        abs_done, wide_col, wide_sum, flag_set = sem("abs_done"), sem("wide_col"), sem("wide_sum"), sem("flag_set")
        wf_ready, wfT_done, wfT_copied = sem("wf_ready"), sem("wfT_done"), sem("wfT_copied")
        gen_bn, gen_xn, gen_xT, gen_xT_copied = sem("gen_bn"), sem("gen_xn"), sem("gen_xT"), sem("gen_xT_copied")
        gen_gu, gen_silu, gen_h, gen_down, gen_y = sem("gen_gu"), sem("gen_silu"), sem("gen_h"), sem("gen_down"), sem("gen_y")

        def x_tile(k, j):
            return xs[:, bass.ds(k * (TILES * D) + j * D, D)]

        gate_up_banks = [gate_ps[0], gate_ps[1], up_ps[0]]
        h32_rows = h32[:].rearrange("p c n -> p (c n)")[:, 0:HC * D]

        T2_ORDER = (1, 0)
        CTX_PARTS = [(0, M), (M, ROWS - M)]
        key_banks = [(gate_ps[0], gate_ps[1], up_ps[0]), (out_ps[0], out_ps[1], up_ps[1])]

        def general_groups():
            flat = "p a b -> p (a b)"
            return ((wg_int[:].rearrange(flat), wgF_T[:].rearrange(flat), [(c * D + d * P) for d in range(DC) for c in range(HC)]),
                    (wu_int[:].rearrange(flat), wuF_T[:].rearrange(flat), [(c * D + d * P) for d in range(DC) for c in range(HC)]),
                    (wd_int[:].rearrange(flat), wdF_T[:].rearrange(flat), [(d * HID + c * P) for c in range(HC) for d in range(DC)]))

        Y_BANKS = (out_ps[0], out_ps[0], out_ps[1], out_ps[1])
        LAST_Y_BANKS = (out_ps[0], out_ps[0], out_ps[1], att_ps[1])
        LAST_TILES = (range(2), range(2, 3), range(3, TILES))
        FAST_STORES = (16 * (BLOCKS // 2 + 1), 16 * (BLOCKS // 2 + len(LAST_TILES)))
        FAST_Y = 4 * BLOCKS + 2

        def weights_are_wide(eng):
            eng.wait_ge(flag_set, 1)
            return eng.value_load(wide_flag[0:1, 0:1], min_val=0, max_val=P) > 0

        block = stack.enter_context(nc.Block())

        @block.sync
        def _(sp):
            def load_x(k, par):
                sp.dma_start(xs[:, bass.ds(k * (TILES * D), TILES * D)], x_v[bass.ds(k, 1)].rearrange("k p f -> (k p) f")).then_inc(x_in[par], 16)

            def store_y(k, par, parts=(range(TILES),)):
                for tiles in parts:
                    lo, hi = tiles[0], tiles[-1] + 1
                    sp.wait_ge(out_free, 4 * k + hi + 2)
                    sp.dma_start(out_v[bass.ds(k, 1), :, lo * D:hi * D].rearrange("k p f -> (k p) f"),
                                 y_sb[:, par, lo * D:hi * D]).then_inc(y_free[par], 16)

            load_x(0, 0)
            sp.dma_start(ctx_nat[:, 1], ctx_rows[:, 1]).then_inc(ctx_in[1], 16)
            load_x(1, 1)
            sp.dma_start(wg_int[:], w_gate.rearrange("(c p) d -> p c d", p=P)).then_inc(wg_in, 16)
            for half in range(2):
                sp.dma_start(ctx_m[half * M:(half + 1) * M].rearrange("m (b d) -> m b d", b=B),
                             ctx.rearrange("b m d -> m b d")).then_inc(ctxm_in, 16)
            sp.dma_start(wu_int[:], w_up.rearrange("(c p) d -> p c d", p=P)).then_inc(wu_in, 16)
            sp.dma_start(wd_int[:], w_down.rearrange("(c p) h -> p c h", p=P)).then_inc(wd_in, 16)
            for par in range(2):
                sp.wait_ge(x_in[par], 16)
                load_x(2 + par, par)

            def step(k, i, par, load):
                if load:
                    sp.wait_ge(x_in[par], 16 * i + 32)
                    load_x(k + 4, par)
                if load or k < BLOCKS - 1:
                    store_y(k, par)
                else:
                    store_y(k, par, LAST_TILES)

            with sp.Fori(0, LOOPS) as i:
                for par in range(2):
                    step(2 * i + par, i, par, True)
            for k in range(2 * LOOPS, BLOCKS):
                step(k, k // 2, k % 2, False)
            for par in range(2):
                sp.wait_ge(y_free[par], FAST_STORES[par])
            with sp.If(weights_are_wide(sp)):
                with sp.Fori(0, BLOCKS) as k:
                    sp.wait_ge(gen_y, 4 * k + 4)
                    sp.dma_start(out_v[bass.ds(k, 1)].rearrange("k p f -> (k p) f"), y_sb[:, 0]).then_inc(y_free[0], 16)
                sp.wait_ge(y_free[0], FAST_STORES[0] + 16 * BLOCKS)

        @block.scalar
        def _(act):
            act.dma_start(W_nat[:], W.rearrange("(c p) d -> p c d", p=P)).then_inc(W_in, 16)
            act.dma_start(ctx_nat[:, 0], ctx_rows[:, 0]).then_inc(ctx_in[0], 16)
            act.dma_start(b_col[:], b.rearrange("(c p) -> p c", p=P), allow_slow_non_contiguous=True).then_inc(b_in, 16)

            act.wait_ge(ones_set, 1)
            nc.scalar.activation(table_probe[:], ones_col[:], ACT.Exp)
            act.dma_start(g_raw[:, 0:1], g_xattn.partition_broadcast(P)).then_inc(g_in, 16)
            act.dma_start(g_raw[:, 1:2], g_ffn.partition_broadcast(P)).then_inc(g_in, 16)

            def copy_t1(a):
                for c in range(DC):
                    act.wait_ge(t1_done, 2 * a + c + 1)
                    nc.scalar.copy(xn1_T[:, c], att_ps[c][:]).then_inc(t1_copied, 1)

            def exp_scores(a):
                act.wait_ge(max_ready, a + 1)
                for j in range(TILES):
                    last = nc.scalar.activation(probs[:, j], scores[:, j], ACT.Exp, bias=neg_max[:, j:j + 1],
                                                accum_out=prob_sum[:, j:j + 1])
                last.then_inc(probs_ready, 1)

            def copy_pt(a):
                act.wait_ge(pt_done, a + 1)
                nc.scalar.copy(probs_T[:], att_ps[1][:]).then_inc(pt_copied, 1)

            def x_high(a):
                for n, c in enumerate(T2_ORDER):
                    act.wait_ge(t2_done, 2 * a + n + 1)
                    nc.scalar.mul(xhi[:, c], att_ps[c][:], LN_SCALE).then_inc(xhi_ready, 1)

            def silu_gate(k, c):
                act.wait_ge(gu_done, 6 * k + c + 1)
                nc.scalar.activation(silu[:, c % 2], gate_ps[c % 2][:], ACT.Silu,
                                     scale=1.0 / (LN_SCALE * QUANT)).then_inc(gate_free, 1)

            def h_high(k, c):
                act.wait_ge(up_free, 6 * k + c + 3)
                nc.scalar.copy(hhi[:, c], h32[:, c]).then_inc(hhi_ready, 1)

            def copy_eo(part):
                act.wait_ge(eo_done, part + 1)
                lo, n = CTX_PARTS[part]
                for e in range(DC):
                    last = nc.scalar.activation(eo_T[:, e, lo:lo + n], key_banks[part][0][:, e * n:(e + 1) * n], ACT.Identity,
                                                bias=b_col[:, e:e + 1])
                last.then_inc(eo_copied, 1)

            def copy_key(part):
                act.wait_ge(key_done, part + 1)
                lo, n = CTX_PARTS[part]
                nc.scalar.copy(key_T[:, :, lo:lo + n], key_banks[part][1][:, 0:DC * n].rearrange("p (c n) -> p c n", c=DC)).then_inc(key_copied, 1)

            def copy_bdot(part):
                act.wait_ge(bdot_done, part + 1)
                lo, n = CTX_PARTS[part]
                nc.scalar.copy(b_dot[:, lo:lo + n], key_banks[part][2][:, 0:n]).then_inc(bdot_copied, 1)

            def copy_wT(dst, banks, done, first):
                for g in range(2):
                    act.wait_ge(wT_done, first + g + 1)
                    nc.scalar.copy(dst(g).bitcast(F32), banks[g][:, 0:HID // 2]).then_inc(done, 1)

            def copy_ctx_T(r, bank):
                act.wait_ge(setup_T, r + 2)
                nc.scalar.copy(ctx_T[:, :, r * P:(r + 1) * P],
                               bank[:, 0:DC * P].rearrange("p (c n) -> p c n", c=DC)).then_inc(ctx_T_copied, 1)

            act.wait_ge(setup_T, 1)
            nc.scalar.copy(W_T[:].rearrange("p c e -> p (c e)"), att_ps[0][:]).then_inc(W_T_copied, 1)
            copy_ctx_T(0, att_ps[1])
            act.wait_ge(b_in, 16)
            copy_eo(0)
            copy_key(0)
            copy_t1(0)
            copy_bdot(0)
            copy_ctx_T(1, up_ps[1])
            act.wait_ge(g_in, 32)
            nc.scalar.activation(g_tanh[:], g_raw[:], ACT.Tanh).then_inc(tanh_done, 1)
            act.wait_ge(wg_in, 16)
            nc.scalar.copy(wg16[:], wg_int[:]).then_inc(wg16_ready, 1)
            exp_scores(0)
            copy_eo(1)
            copy_pt(0)
            copy_wT(lambda g: wg_T[:, g], gate_ps, gate_free, 0)
            act.wait_ge(wd_in, 16)
            nc.scalar.copy(wd16[:], wd_int[:]).then_inc(wd16_ready, 1)
            copy_key(1)
            copy_t1(1)
            copy_bdot(1)
            copy_wT(lambda g: wu_T[:, g], up_ps, up_free, 2)
            copy_wT(lambda g: wd_T[:, g * (HC // 2):(g + 1) * (HC // 2)].rearrange("p c d -> p (c d)"), out_ps, out_free, 4)
            x_high(0)
            exp_scores(1)

            def step(k, next1, next2):
                silu_gate(k, 0)
                silu_gate(k, 1)
                h_high(k, 0)
                if next1:
                    copy_pt(k + 1)
                silu_gate(k, 2)
                h_high(k, 1)
                silu_gate(k, 3)
                h_high(k, 2)
                silu_gate(k, 4)
                h_high(k, 3)
                if next2:
                    copy_t1(k + 2)
                silu_gate(k, 5)
                h_high(k, 4)
                h_high(k, 5)
                if next1:
                    x_high(k + 1)
                if next2:
                    exp_scores(k + 2)

            with act.Fori(0, LOOPS) as i:
                for par in range(2):
                    step(2 * i + par, True, True)
            for k in range(2 * LOOPS, BLOCKS):
                step(k, k + 1 < BLOCKS, k + 2 < BLOCKS)

            with act.If(weights_are_wide(act)):
                act.wait_ge(out_free, FAST_Y)
                with act.Fori(0, BLOCKS) as k:
                    for j in range(TILES):
                        act.wait_ge(gen_gu, 4 * k + j + 1)
                        for g, (bank, n) in enumerate(zip(gate_ps, (512, HID - 512))):
                            last = nc.scalar.activation(silu[:].rearrange("p a n -> p (a n)")[:, g * 512:g * 512 + n],
                                                        bank[:, 0:n], ACT.Silu)
                        last.then_inc(gen_silu, 1)

        @block.gpsimd
        def _(pool):
            nc.gpsimd.memset(ident[:], 0.0).then_inc(ident_set, 1)
            pool.wait_ge(ident_set, 1)
            nc.gpsimd.affine_select(out=ident[:], in_=ident[:], compare_op=ALU.not_equal, fill=1.0, base=0,
                                    pattern=[[-1, P]], channel_multiplier=1).then_inc(ident_set, 1)
            pool.wait_ge(ident_set, 2)
            nc.gpsimd.tensor_copy(ident16[:], ident[:]).then_inc(ident_set, 1)

            def h_low(k, c):
                pool.wait_ge(hhi_ready, 6 * k + c + 1)
                nc.gpsimd.tensor_tensor(hlo[:, c], h32[:, c], hhi[:, c], ALU.subtract).then_inc(hlo_ready, 1)

            pool.wait_ge(b_in, 16)
            for c in range(DC):
                nc.gpsimd.tensor_copy(b_rep[:, c], b_col[:, c:c + 1].broadcast_to([P, P])).then_inc(b_rep_set, 1)
            pool.wait_ge(ctxm_in, 32)
            nc.gpsimd.tensor_copy(ctx_hi[:], ctx_m[:]).then_inc(ctx_split, 1)
            pool.wait_ge(ctx_split, 1)
            nc.gpsimd.tensor_tensor(ctx_lo[:], ctx_m[:], ctx_hi[:].bitcast(F32), ALU.subtract).then_inc(ctx_split, 1)
            pool.wait_ge(wu_in, 16)
            nc.gpsimd.tensor_copy(wu16[:], wu_int[:]).then_inc(wu16_ready, 1)

            with pool.Fori(0, BLOCKS) as k:
                for c in range(HC):
                    h_low(k, c)

        @block.vector
        def _(dve):
            def norm_stats(k, w):
                for j in range(TILES):
                    last = nc.vector.bn_stats(stats[:, w, j], x_tile(k, j))
                last.then_inc(bn_done, 1)

            def norm_factors(m, half, stats_needed, stats_sem=bn_done):
                n = LN_OPS * m
                even, odd = stats[:, half, :, 0:3], stats[:, half, :, 3:6]
                v = nc.vector
                dve.wait_ge(stats_sem, stats_needed)
                v.tensor_tensor(mean_sum[:, half], even[:, :, :, 1], odd[:, :, :, 1], ALU.add).then_inc(ln_math, 1)
                v.tensor_tensor(mean_gap[:, half], even[:, :, :, 1], odd[:, :, :, 1], ALU.subtract).then_inc(ln_math, 1)
                v.scalar_tensor_tensor(out=sq_sum[:, half], in0=even[:, :, :, 2], scalar=EPS * D, in1=odd[:, :, :, 2],
                                       op0=ALU.add, op1=ALU.add).then_inc(ln_math, 1)
                dve.wait_ge(ln_math, n + 2)
                v.scalar_tensor_tensor(out=gap_sq[:, half], in0=mean_gap[:, half], scalar=0.25, in1=mean_gap[:, half],
                                       op0=ALU.mult, op1=ALU.mult).then_inc(ln_math, 1)
                v.tensor_scalar(mean[:, half], mean_sum[:, half], 0.5, None, ALU.mult).then_inc(ln_math, 1)
                dve.wait_ge(ln_math, n + 4)
                v.scalar_tensor_tensor(out=var_eps[:, half], in0=sq_sum[:, half], scalar=1.0 / D, in1=gap_sq[:, half],
                                       op0=ALU.mult, op1=ALU.add).then_inc(ln_math, 1)
                dve.wait_ge(ln_math, n + 6)
                v.tensor_scalar(rsqrt[:, 0, half].bitcast(I32), var_eps[:, half].bitcast(I32), -0.5, RSQRT_MAGIC,
                                ALU.mult, ALU.add).then_inc(ln_math, 1)
                for t in range(NEWTON):
                    y = rsqrt[:, t, half]
                    dve.wait_ge(ln_math, n + 7 + 3 * t)
                    v.tensor_tensor(rsqrt_sq[:, t, half], y, y, ALU.mult).then_inc(ln_math, 1)
                    dve.wait_ge(ln_math, n + 8 + 3 * t)
                    v.scalar_tensor_tensor(out=rsqrt_res[:, t, half], in0=rsqrt_sq[:, t, half], scalar=-0.5,
                                           in1=var_eps[:, half], op0=ALU.mult, op1=ALU.mult).then_inc(ln_math, 1)
                    dve.wait_ge(ln_math, n + 9 + 3 * t)
                    v.scalar_tensor_tensor(out=rsqrt[:, t + 1, half], in0=rsqrt_res[:, t, half], scalar=1.5, in1=y,
                                           op0=ALU.add, op1=ALU.mult).then_inc(ln_math, 1)

            def normalise(k, dst, m, w, ready):
                dve.wait_ge(ln_math, LN_OPS * (m + 1))
                for j in range(TILES):
                    last = nc.vector.tensor_scalar(dst[:, j], x_tile(k, j), mean[:, w, j:j + 1],
                                                   rsqrt[:, NEWTON, w, j:j + 1], ALU.subtract, ALU.mult)
                last.then_inc(ready, 1)

            def row_max(a, batch):
                dve.wait_ge(s_done, a + 1)
                bd = b_dot[:, bass.ds(batch * M, M)].unsqueeze(1).broadcast_to([P, TILES, M])
                nc.vector.tensor_tensor(scores[:], att_ps[0][:, 0:TILES * M].rearrange("p (j m) -> p j m", j=TILES),
                                        bd, ALU.add).then_inc(s_added, 1)
                dve.wait_ge(s_added, a + 1)
                nc.vector.tensor_reduce(neg_max[:], scores[:], AX.X, ALU.max, negate=True).then_inc(max_ready, 1)

            def split_probs(a):
                dve.wait_ge(probs_ready, a + 1)
                nc.vector.tensor_copy(probs_hl[:, :, 0], probs[:]).then_inc(phi_ready, 1)
                dve.wait_ge(phi_ready, a + 1)
                nc.vector.tensor_tensor(probs_hl[:, :, 1], probs[:], probs_hl[:, :, 0].bitcast(F32),
                                        ALU.subtract).then_inc(plo_ready, 1)
                nc.vector.reciprocal(prob_rcp[:], prob_sum[:]).then_inc(rcp_done, 1)
                dve.wait_ge(rcp_done, a + 1)
                nc.vector.tensor_scalar(attn_coef[:], prob_rcp[:], g_tanh[:, 0:1], None, ALU.mult).then_inc(acoef_ready, 1)

            def add_attention(a):
                dve.wait_ge(acoef_ready, a + 1)
                for j in range(TILES):
                    if j % 2 == 0:
                        dve.wait_ge(pv_done, 2 * a + j // 2 + 1)
                    last = nc.vector.scalar_tensor_tensor(out=x_tile(a, j), in0=att_ps[j // 2][:, (j % 2) * D:(j % 2 + 1) * D],
                                                          scalar=attn_coef[:, j:j + 1], in1=x_tile(a, j),
                                                          op0=ALU.mult, op1=ALU.add)
                last.then_inc(x1_ready, 1)

            def x_low(a):
                for n, c in enumerate(T2_ORDER):
                    dve.wait_ge(xhi_ready, 2 * a + n + 1)
                    nc.vector.scalar_tensor_tensor(out=xlo[:, c], in0=att_ps[c][:], scalar=LN_SCALE, in1=xhi[:, c],
                                                   op0=ALU.mult, op1=ALU.subtract).then_inc(xlo_ready, 1)

            def h_of(k, c):
                dve.wait_ge(gate_free, 6 * k + c + 3)
                nc.vector.scalar_tensor_tensor(out=h32[:, c], in0=up_ps[c % 2][:], scalar=H_SCALE / (LN_SCALE * QUANT),
                                               in1=silu[:, c % 2], op0=ALU.mult, op1=ALU.mult).then_inc(up_free, 1)

            def add_ffn(k, i, par, y_banks=Y_BANKS):
                banks_done = 0
                dve.wait_ge(y_free[par], 16 * i + 16)
                for j in range(TILES):
                    bank = y_banks[j]
                    if j == 0 or bank is not y_banks[j - 1]:
                        banks_done += 1
                        dve.wait_ge(down_done, 2 * k + banks_done)
                    nc.vector.scalar_tensor_tensor(out=y_sb[:, par, j * D:(j + 1) * D],
                                                   in0=bank[:, (j % 2) * D:(j % 2 + 1) * D],
                                                   scalar=out_coef[:, 0:1], in1=x_tile(k, j),
                                                   op0=ALU.mult, op1=ALU.add).then_inc(out_free, 1)

            nc.vector.memset(ones_col[:], 1.0).then_inc(ones_set, 1)
            for half in range(2):
                nc.vector.memset(y_sb[:, half, 0:1], 0.0).then_inc(y_free[half], 16)
            dve.wait_ge(x_in[0], 16)
            norm_stats(0, 0)
            norm_factors(0, slice(0, 1), 1)
            normalise(0, xn1, 0, 0, xn1_ready)
            dve.wait_ge(x_in[1], 16)
            norm_stats(1, 0)
            norm_factors(1, slice(0, 1), 2)
            dve.wait_ge(bdot_copied, 1)
            row_max(0, 0)
            dve.wait_ge(t1_done, 2)
            normalise(1, xn1, 1, 0, xn1_ready)
            dve.wait_ge(tanh_done, 1)
            nc.vector.tensor_scalar(out_coef[:], g_tanh[:, 1:2], 1.0 / (H_SCALE * QUANT), None, ALU.mult).then_inc(coef_done, 1)
            split_probs(0)
            dve.wait_ge(x_in[0], 32)
            norm_stats(2, 0)
            add_attention(0)
            dve.wait_ge(x1_ready, 1)
            norm_stats(0, 1)
            norm_factors(2, slice(0, 2), 4)
            normalise(0, xn2, 2, 1, xn2_ready)
            row_max(1, 0)
            x_low(0)
            normalise(2, xn1, 2, 0, xn1_ready)
            dve.wait_ge(coef_done, 1)
            dve.wait_ge(bdot_copied, 2)

            def largest_weight(n):
                w_int = (wg_int, wu_int, wd_int)[n]
                nc.vector.tensor_reduce(w_abs[:, n:n + 1], w_int[:], AX.XY, ALU.max, apply_absolute_value=True).then_inc(abs_done, 1)

            def find_wide_weights():
                dve.wait_ge(abs_done, 3)
                nc.vector.tensor_reduce(w_max[:], w_abs[:], AX.X, ALU.max).then_inc(abs_done, 1)
                dve.wait_ge(abs_done, 4)
                nc.vector.tensor_scalar(w_wide[:], w_max[:], QUANT, None, ALU.is_gt).then_inc(wide_col, 1)

            def step(k, i, par, batch2, next1, next2, next3, bn_count):
                if next1:
                    split_probs(k + 1)
                h_of(k, 0)
                if next3:
                    dve.wait_ge(x_in[1 - par], 16 * (i + par) + 32)
                h_of(k, 1)
                if next3:
                    norm_stats(k + 3, 0)
                elif next1:
                    largest_weight(0 if next2 else 2)
                else:
                    find_wide_weights()
                h_of(k, 2)
                if next1:
                    add_attention(k + 1)
                    dve.wait_ge(x1_ready, k + 2)
                h_of(k, 3)
                if next1:
                    norm_stats(k + 1, 1)
                h_of(k, 4)
                if next1:
                    norm_factors(k + 3, slice(0 if next3 else 1, 2), bn_count)
                h_of(k, 5)
                if next1:
                    normalise(k + 1, xn2, k + 3, 1, xn2_ready)
                if next2:
                    row_max(k + 2, batch2)
                if next1:
                    x_low(k + 1)
                else:
                    dve.wait_ge(wide_sum, 1)
                    nc.vector.tensor_copy(wide_flag[:], att_ps[0][0:1, 0:1]).then_inc(flag_set, 1)
                if next3:
                    normalise(k + 3, xn1, k + 3, 0, xn1_ready)
                elif next2:
                    largest_weight(1)
                add_ffn(k, i, par, Y_BANKS if next1 else LAST_Y_BANKS)

            with dve.Fori(0, LOOPS) as i:
                for par in range(2):
                    step(2 * i + par, i, par, i + 1, True, True, True, 4 * i + 2 * par + 6)
            for k in range(2 * LOOPS, BLOCKS):
                bn_count = sum(a + 3 < BLOCKS for a in range(k + 1)) + sum(a + 1 < BLOCKS for a in range(k + 1)) + 4
                step(k, k // 2, k % 2, k // 2 + 1, k + 1 < BLOCKS, k + 2 < BLOCKS, k + 3 < BLOCKS, bn_count)

            with dve.If(weights_are_wide(dve)):
                dve.wait_ge(out_free, FAST_Y)
                groups = general_groups()
                for n, (w_int, _, _) in enumerate(groups):
                    if n:
                        dve.wait_ge(wfT_done, 3 * n)
                    nc.vector.tensor_scalar(h32_rows, w_int, 1.0 / QUANT, None, ALU.mult).then_inc(wf_ready, 1)
                    for g in range(3):
                        dve.wait_ge(wfT_done, 3 * n + g + 1)
                        nc.vector.tensor_copy(groups[n][1][:, g * 512:(g + 1) * 512], gate_up_banks[g][:]).then_inc(wfT_copied, 1)

                def general_tile(k, j):
                    t = 4 * k + j
                    nc.vector.bn_stats(stats[:, 0, 0], x_tile(k, j)).then_inc(gen_bn, 1)
                    norm_factors(BLOCKS + 2 + t, slice(0, 1), t + 1, gen_bn)
                    dve.wait_ge(ln_math, LN_OPS * (BLOCKS + 3 + t))
                    nc.vector.tensor_scalar(xn1[:, 0], x_tile(k, j), mean[:, 0, 0:1], rsqrt[:, NEWTON, 0, 0:1],
                                            ALU.subtract, ALU.mult).then_inc(gen_xn, 1)
                    dve.wait_ge(gen_xT, t + 1)
                    nc.vector.tensor_copy(xn1_T[:, 0, 0:D], att_ps[0][:, 0:D]).then_inc(gen_xT_copied, 1)
                    dve.wait_ge(gen_silu, t + 1)
                    for g, (bank, n) in enumerate(zip(up_ps, (512, HID - 512))):
                        last = nc.vector.tensor_tensor(h32[:].rearrange("p c n -> p (c n)")[:, g * 512:g * 512 + n], bank[:, 0:n],
                                                       silu[:].rearrange("p a n -> p (a n)")[:, g * 512:g * 512 + n], ALU.mult)
                    last.then_inc(gen_h, 1)
                    if j == 0:
                        dve.wait_ge(y_free[0], 16 * k + FAST_STORES[0])
                    dve.wait_ge(gen_down, t + 1)
                    nc.vector.scalar_tensor_tensor(out=y_sb[:, 0, j * D:(j + 1) * D], in0=out_ps[0][:, 0:D],
                                                   scalar=g_tanh[:, 1:2], in1=x_tile(k, j), op0=ALU.mult, op1=ALU.add).then_inc(gen_y, 1)

                with dve.Fori(0, BLOCKS) as k:
                    for j in range(TILES):
                        general_tile(k, j)

        @block.tensor
        def _(pe):
            mm = nc.tensor.matmul

            def t1(a, after_attention=True):
                if after_attention:
                    pe.wait_ge(x1_ready, a)
                pe.wait_ge(xn1_ready, a + 1)
                for c in range(DC):
                    for j in range(TILES):
                        last = nc.tensor.transpose(att_ps[c][:, j * P:(j + 1) * P], xn1[:, j, c * P:(c + 1) * P], ident[:])
                    last.then_inc(t1_done, 1)

            def score(a, batch):
                pe.wait_ge(t1_copied, 2 * a + 2)
                for j in range(TILES):
                    for c in range(DC):
                        last = mm(att_ps[0][:, j * M:(j + 1) * M], xn1_T[:, c, j * P:(j + 1) * P],
                                  key_T[:, c, bass.ds(batch * M, M)], start=(c == 0), stop=(c == DC - 1))
                last.then_inc(s_done, 1)

            def transpose_probs(a):
                pe.wait_ge(plo_ready, a + 1)
                for j in range(TILES):
                    last = nc.tensor.transpose(att_ps[1][:, j * P:(j + 1) * P],
                                               probs_hl[:, j].rearrange("p h m -> p (h m)").bitcast(F32), ident[:])
                last.then_inc(pt_done, 1)

            def attend(a, batch):
                pe.wait_ge(pt_copied, a + 1)
                for j in range(TILES):
                    for n, c_half in enumerate((ctx_hi, ctx_lo)):
                        last = mm(att_ps[j // 2][:, (j % 2) * D:(j % 2 + 1) * D], probs_T[:, j * P:(j + 1) * P],
                                  c_half[:, bass.ds(batch * D, D)], start=(n == 0), stop=(n == 1))
                    if j % 2 == 1:
                        last.then_inc(pv_done, 1)

            def t2(a, after_score=True):
                pe.wait_ge(xn2_ready, a + 1)
                for c in T2_ORDER:
                    if c == 0 and after_score:
                        pe.wait_ge(s_added, a + 2)
                    for j in range(TILES):
                        last = nc.tensor.transpose(att_ps[c][:, j * P:(j + 1) * P], xn2[:, j, c * P:(c + 1) * P], ident[:])
                    last.then_inc(t2_done, 1)

            def gate_up(k, c):
                pe.wait_ge(gate_free, 6 * k + c + 1)
                pe.wait_ge(up_free, 6 * k + c + 1)
                for n, half in enumerate((xhi, xlo)):
                    for w_T, bank in ((wg_T, gate_ps[c % 2]), (wu_T, up_ps[c % 2])):
                        for i, d in enumerate(T2_ORDER):
                            if c == 0 and w_T is wg_T:
                                pe.wait_ge((xhi_ready, xlo_ready)[n], 2 * k + i + 1)
                            last = mm(bank[:], w_T[:, d, c * P:(c + 1) * P], half[:, d],
                                      start=(n == 0 and i == 0), stop=(n == 1 and i == DC - 1))
                last.then_inc(gu_done, 1)

            def down(k, c, tiles=range(TILES), y_banks=Y_BANKS):
                if c == 0:
                    pe.wait_ge(out_free, 4 * k + 2)
                pe.wait_ge(hlo_ready, 6 * k + c + 1)
                for j in tiles:
                    bank = y_banks[j]
                    first = j == 0 or bank is not y_banks[j - 1]
                    for n, half in enumerate((hhi, hlo)):
                        last = mm(bank[:, (j % 2) * D:(j % 2 + 1) * D], half[:, c, j * P:(j + 1) * P], wd_T[:, c],
                                  start=(c == 0 and n == 0 and first), stop=(c == HC - 1 and n == 1),
                                  skip_group_check=True)
                    if c == HC - 1 and (j == TILES - 1 or bank is not y_banks[j + 1]):
                        last.then_inc(down_done, 1)

            def context_out(part):
                lo, n = CTX_PARTS[part]
                for e in range(DC):
                    for d in range(DC):
                        last = mm(key_banks[part][0][:, e * n:(e + 1) * n], W_T[:, d, e * P:(e + 1) * P], ctx_T[:, d, lo:lo + n],
                                  start=(d == 0), stop=(d == DC - 1))
                last.then_inc(eo_done, 1)

            def keys(part):
                pe.wait_ge(eo_copied, part + 1)
                lo, n = CTX_PARTS[part]
                for d in range(DC):
                    for e in range(DC):
                        last = mm(key_banks[part][1][:, d * n:(d + 1) * n], W_nat[:, e, d * P:(d + 1) * P], eo_T[:, e, lo:lo + n],
                                  start=(e == 0), stop=(e == DC - 1))
                last.then_inc(key_done, 1)

            def b_dots(part):
                lo, n = CTX_PARTS[part]
                for e in range(DC):
                    last = mm(key_banks[part][2][:, 0:n], b_rep[:, e], eo_T[:, e, lo:lo + n], start=(e == 0), stop=(e == DC - 1))
                last.then_inc(bdot_done, 1)

            def transpose_gate_or_up(w16, banks, ready):
                pe.wait_ge(ident_set, 3)
                pe.wait_ge(ready, 1)
                for d in range(DC):
                    o = banks[d][:].bitcast(F16)
                    for c in range(HC):
                        last = nc.tensor.transpose(o[:, c * P:(c + 1) * P], w16[:, c, d * P:(d + 1) * P], ident16[:])
                    last.then_inc(wT_done, 1)

            def transpose_down():
                pe.wait_ge(wd16_ready, 1)
                for g in range(2):
                    o = out_ps[g][:].bitcast(F16)
                    for c in range(HC // 2):
                        for d in range(DC):
                            h0 = (g * (HC // 2) + c) * P
                            last = nc.tensor.transpose(o[:, (c * DC + d) * P:(c * DC + d + 1) * P], wd16[:, d, h0:h0 + P], ident16[:])
                    last.then_inc(wT_done, 1)

            def keep_warm(n):
                for _ in range(n):
                    nc.tensor.transpose(out_ps[1][:, 0:P], ident[:], ident[:])

            pe.wait_ge(ident_set, 2)
            keep_warm(15)
            pe.wait_ge(W_in, 16)
            for d in range(DC):
                for c in range(DC):
                    o = d * D + c * P
                    last = nc.tensor.transpose(att_ps[0][:, o:o + P], W_nat[:, c, d * P:(d + 1) * P], ident[:])
            last.then_inc(setup_T, 1)

            def transpose_ctx(r, bank):
                pe.wait_ge(ctx_in[r], 16)
                for d in range(DC):
                    last = nc.tensor.transpose(bank[:, d * P:(d + 1) * P], ctx_nat[:, r, d * P:(d + 1) * P], ident[:])
                last.then_inc(setup_T, 1)

            transpose_ctx(0, att_ps[1])
            keep_warm(5)
            pe.wait_ge(W_T_copied, 1)
            pe.wait_ge(ctx_T_copied, 1)
            context_out(0)
            keep_warm(4)
            keys(0)
            t1(0, False)
            pe.wait_ge(b_rep_set, 2)
            b_dots(0)
            transpose_ctx(1, up_ps[1])
            pe.wait_ge(key_copied, 1)
            score(0, 0)
            pe.wait_ge(ctx_T_copied, 2)
            context_out(1)
            transpose_probs(0)
            transpose_gate_or_up(wg16, gate_ps, wg16_ready)
            pe.wait_ge(ctx_split, 2)
            attend(0, 0)
            keys(1)
            t1(1)
            b_dots(1)
            score(1, 0)
            pe.wait_ge(bdot_copied, 2)
            transpose_gate_or_up(wu16, up_ps, wu16_ready)
            transpose_down()
            t2(0)

            def step(k, batch1, batch2, next1, next2):
                gate_up(k, 0)
                gate_up(k, 1)
                if next1:
                    transpose_probs(k + 1)
                gate_up(k, 2)
                if next1:
                    attend(k + 1, batch1)
                gate_up(k, 3)
                if not next1:
                    pe.wait_ge(wide_col, 1)
                    pe.wait_ge(ones_set, 1)
                    mm(att_ps[0][0:1, 0:1], w_wide[:], ones_col[:], start=True, stop=True).then_inc(wide_sum, 1)
                gate_up(k, 4)
                if next2:
                    t1(k + 2)
                gate_up(k, 5)
                if next2:
                    score(k + 2, batch2)
                if next1:
                    before_t2 = 3 if next2 else 5
                    for c in range(before_t2):
                        down(k, c)
                    t2(k + 1, next2)
                    for c in range(before_t2, HC):
                        down(k, c)
                else:
                    for c in range(3):
                        down(k, c, y_banks=LAST_Y_BANKS)
                    for tiles in LAST_TILES:
                        for c in range(3, HC):
                            down(k, c, tiles, LAST_Y_BANKS)

            with pe.Fori(0, LOOPS) as i:
                for par in range(2):
                    step(2 * i + par, i + par, i + 1, True, True)
            for k in range(2 * LOOPS, BLOCKS):
                step(k, (k + 1) // 2, k // 2 + 1, k + 1 < BLOCKS, k + 2 < BLOCKS)

            with pe.If(weights_are_wide(pe)):
                pe.wait_ge(out_free, FAST_Y)
                for n, (_, _, blocks) in enumerate(general_groups()):
                    pe.wait_ge(wf_ready, n + 1)
                    for g in range(3):
                        if n:
                            pe.wait_ge(wfT_copied, 3 * (n - 1) + g + 1)
                        for q in range(4):
                            at = blocks[4 * g + q]
                            last = nc.tensor.transpose(gate_up_banks[g][:, q * P:(q + 1) * P], h32_rows[:, at:at + P], ident[:])
                        last.then_inc(wfT_done, 1)
                pe.wait_ge(wfT_copied, 9)
                with pe.Fori(0, BLOCKS) as k:
                    for j in range(TILES):
                        t = 4 * k + j
                        pe.wait_ge(gen_xn, t + 1)
                        for d in range(DC):
                            last = nc.tensor.transpose(att_ps[0][:, d * P:(d + 1) * P], xn1[:, 0, d * P:(d + 1) * P], ident[:])
                        last.then_inc(gen_xT, 1)
                        pe.wait_ge(gen_xT_copied, t + 1)
                        for w_T, banks in ((wgF_T, gate_ps), (wuF_T, up_ps)):
                            for c in range(HC):
                                for d in range(DC):
                                    last = mm(banks[c // 4][:, c % 4 * P:(c % 4 + 1) * P], w_T[:, d, c * P:(c + 1) * P],
                                              xn1_T[:, 0, d * P:(d + 1) * P], start=(d == 0), stop=(d == DC - 1))
                        last.then_inc(gen_gu, 1)
                        pe.wait_ge(gen_h, t + 1)
                        for c in range(HC):
                            last = mm(out_ps[0][:, 0:D], h32[:].rearrange("p c n -> p (c n)")[:, c * P:(c + 1) * P], wdF_T[:, c],
                                      start=(c == 0), stop=(c == HC - 1))
                        last.then_inc(gen_down, 1)


_INS = ["x", "ctx_1024", "g_xattn", "g_ffn", "L0_xattn_W", "L0_xattn_b", "L0_ffn_w_gate", "L0_ffn_w_up", "L0_ffn_w_down"]


def kernel(**inputs):
    import numpy as np
    import concourse.bacc as bacc
    from concourse import mybir as mb
    from concourse.bass_utils import run_bass_kernel_spmd as run

    nc = bacc.Bacc("TRN2", target_bir_lowering=False, num_devices=1)
    arrays, args = {}, []
    for name in _INS:
        a = np.ascontiguousarray(inputs[name])
        arrays[f"in_{name}"] = a
        args.append(nc.dram_tensor(f"in_{name}", a.shape, mb.dt.from_np(a.dtype), kind="ExternalInput").ap())
    x = arrays["in_x"]
    o = nc.dram_tensor("out_y", x.shape, mb.dt.float32, kind="ExternalOutput").ap()
    gated_cross_attention_and_ffn(nc, *args, o)
    r = run(nc, [arrays], core_ids=[0])
    return r.results[0]["out_y"]
```
